# Optimizing a Trainium2 kernel written in Bass

```python
import numpy as np
import jax
import jax.numpy as jnp

def _softmax(x, axis=-1):
    return jax.nn.softmax(x, axis=axis)

def _gelu(x):
    return jax.nn.gelu(x, approximate=True)

def _silu(x):
    return jax.nn.silu(x)

def _sigmoid(x):
    return jax.nn.sigmoid(x)

def _layernorm(x, axis=-1, eps=1e-05):
    m = jnp.mean(x, axis=axis, keepdims=True)
    v = jnp.var(x, axis=axis, keepdims=True)
    return (x - m) / jnp.sqrt(v + eps)

def _scatter_add(tgt, idx, src, axis=0):
    return tgt.at[idx].add(src)

def _segment_sum(src, seg, n):
    return jax.ops.segment_sum(src, seg, n)
kernel_name = 'mk_gnn_resnorm_d1_gnn_r32_d9e19a'

def setup_inputs(seed: int=0):
    np.random.seed(seed)
    _w = jnp.asarray

    def _rec_inputs():
        import jax
        import jax.numpy as jnp
        _gk = jax.random.key(seed)
        x = -0.000202 + 1 * jax.random.normal(jax.random.fold_in(_gk, 1), (3125, 128), jnp.float32)
        src = jax.random.randint(jax.random.fold_in(_gk, 2), (50000,), 0, 3125, jnp.int32)
        dst = jnp.minimum((3125 * jax.random.uniform(jax.random.fold_in(_gk, 3), (50000,)) ** 2.0).astype(jnp.int32), 99999)
        _o = jnp.argsort(dst, stable=True)
        src = src[_o]
        dst = dst[_o]
        return (x, src, dst)
    x, src, dst = _rec_inputs()

    def _L0_gnn_setup():
        import jax, jax.numpy as jnp
        import numpy as np
        N_NODES = 50000
        N_EDGES = 9375
        HIDDEN = 128
        HEADS = 2

        def _lin_params(key, fan_in, fan_out):
            k1, k2 = jax.random.split(key)
            s = 1.0 / np.sqrt(fan_in)
            w = jax.random.uniform(k1, (fan_in, fan_out), jnp.float32, -s, s)
            b = jax.random.uniform(k2, (fan_out,), jnp.float32, -s, s)
            return (w, b)

        def _transformer_conv(x, src, dst, qw, qb, kw, kb, vw, vb, sw, sb):
            N = x.shape[0]
            H, D = (HEADS, HIDDEN)
            q = (x @ qw + qb).reshape(N, H, D)
            k = (x @ kw + kb).reshape(N, H, D)
            v = (x @ vw + vb).reshape(N, H, D)
            scale = 1.0 / jnp.sqrt(jnp.float32(D))
            alpha = jnp.einsum('ehd,ehd->eh', q[dst], k[src]) * scale
            m = jax.ops.segment_max(alpha, dst, num_segments=N)
            ex = jnp.exp(alpha - m[dst])
            denom = jax.ops.segment_sum(ex, dst, num_segments=N)
            w = ex / (denom[dst] + 1e-16)
            agg = jax.ops.segment_sum(w[:, :, None] * v[src], dst, num_segments=N)
            return agg.mean(axis=1) + x @ sw + sb
        key = jax.random.key(seed)
        keys = jax.random.split(key, 16)
        x = jax.random.normal(keys[0], (N_NODES, HIDDEN), jnp.float32)
        edge_index = jax.random.randint(keys[1], (2, N_EDGES), 0, N_NODES, jnp.int32)
        inp = {'x': x, 'edge_index': edge_index}
        names = ['q1', 'k1', 'v1', 's1', 'q2', 'k2', 'v2', 's2', 'lin1', 'lin2']
        outs = [HEADS * HIDDEN] * 3 + [HIDDEN] + [HEADS * HIDDEN] * 3 + [HIDDEN, HIDDEN, HIDDEN]
        for i, (nm, fo) in enumerate(zip(names, outs)):
            w, b = _lin_params(keys[2 + i], HIDDEN, fo)
            inp[nm + '_w'] = w
            inp[nm + '_b'] = b
        return inp
    _L0_gnn_all = _L0_gnn_setup()
    _L0_gnn_in = {k: v for k, v in _L0_gnn_all.items() if k in ('q1_w', 'q1_b', 'k1_w', 'k1_b', 'v1_w', 'v1_b', 's1_w', 's1_b', 'q2_w', 'q2_b', 'k2_w', 'k2_b', 'v2_w', 'v2_b', 's2_w', 's2_b', 'lin1_w', 'lin1_b', 'lin2_w', 'lin2_b')}
    del _L0_gnn_all
    return {'x': x, 'src': src, 'dst': dst, 'L0_gnn_q1_w': _L0_gnn_in['q1_w'], 'L0_gnn_q1_b': _L0_gnn_in['q1_b'], 'L0_gnn_k1_w': _L0_gnn_in['k1_w'], 'L0_gnn_k1_b': _L0_gnn_in['k1_b'], 'L0_gnn_v1_w': _L0_gnn_in['v1_w'], 'L0_gnn_v1_b': _L0_gnn_in['v1_b'], 'L0_gnn_s1_w': _L0_gnn_in['s1_w'], 'L0_gnn_s1_b': _L0_gnn_in['s1_b'], 'L0_gnn_q2_w': _L0_gnn_in['q2_w'], 'L0_gnn_q2_b': _L0_gnn_in['q2_b'], 'L0_gnn_k2_w': _L0_gnn_in['k2_w'], 'L0_gnn_k2_b': _L0_gnn_in['k2_b'], 'L0_gnn_v2_w': _L0_gnn_in['v2_w'], 'L0_gnn_v2_b': _L0_gnn_in['v2_b'], 'L0_gnn_s2_w': _L0_gnn_in['s2_w'], 'L0_gnn_s2_b': _L0_gnn_in['s2_b'], 'L0_gnn_lin1_w': _L0_gnn_in['lin1_w'], 'L0_gnn_lin1_b': _L0_gnn_in['lin1_b'], 'L0_gnn_lin2_w': _L0_gnn_in['lin2_w'], 'L0_gnn_lin2_b': _L0_gnn_in['lin2_b']}

def reference(x, src, dst, L0_gnn_q1_w, L0_gnn_q1_b, L0_gnn_k1_w, L0_gnn_k1_b, L0_gnn_v1_w, L0_gnn_v1_b, L0_gnn_s1_w, L0_gnn_s1_b, L0_gnn_q2_w, L0_gnn_q2_b, L0_gnn_k2_w, L0_gnn_k2_b, L0_gnn_v2_w, L0_gnn_v2_b, L0_gnn_s2_w, L0_gnn_s2_b, L0_gnn_lin1_w, L0_gnn_lin1_b, L0_gnn_lin2_w, L0_gnn_lin2_b):
    import jax
    import jax.numpy as jnp

    def _L0_gnn_ref(x, edge_index, q1_w, q1_b, k1_w, k1_b, v1_w, v1_b, s1_w, s1_b, q2_w, q2_b, k2_w, k2_b, v2_w, v2_b, s2_w, s2_b, lin1_w, lin1_b, lin2_w, lin2_b):
        import jax, jax.numpy as jnp
        import numpy as np
        N_NODES = 50000
        N_EDGES = 9375
        HIDDEN = 128
        HEADS = 2

        def _lin_params(key, fan_in, fan_out):
            k1, k2 = jax.random.split(key)
            s = 1.0 / np.sqrt(fan_in)
            w = jax.random.uniform(k1, (fan_in, fan_out), jnp.float32, -s, s)
            b = jax.random.uniform(k2, (fan_out,), jnp.float32, -s, s)
            return (w, b)

        def _transformer_conv(x, src, dst, qw, qb, kw, kb, vw, vb, sw, sb):
            N = x.shape[0]
            H, D = (HEADS, HIDDEN)
            q = (x @ qw + qb).reshape(N, H, D)
            k = (x @ kw + kb).reshape(N, H, D)
            v = (x @ vw + vb).reshape(N, H, D)
            scale = 1.0 / jnp.sqrt(jnp.float32(D))
            alpha = jnp.einsum('ehd,ehd->eh', q[dst], k[src]) * scale
            m = jax.ops.segment_max(alpha, dst, num_segments=N)
            ex = jnp.exp(alpha - m[dst])
            denom = jax.ops.segment_sum(ex, dst, num_segments=N)
            w = ex / (denom[dst] + 1e-16)
            agg = jax.ops.segment_sum(w[:, :, None] * v[src], dst, num_segments=N)
            return agg.mean(axis=1) + x @ sw + sb
        src, dst = (edge_index[0], edge_index[1])
        h = _transformer_conv(x, src, dst, q1_w, q1_b, k1_w, k1_b, v1_w, v1_b, s1_w, s1_b)
        h = h + x @ lin1_w + lin1_b
        out = _transformer_conv(h, src, dst, q2_w, q2_b, k2_w, k2_b, v2_w, v2_b, s2_w, s2_b)
        out = out + h @ lin2_w + lin2_b
        return out
    edge_index = jnp.stack([src, dst])
    x = _layernorm(x + _L0_gnn_ref(x, edge_index, L0_gnn_q1_w, L0_gnn_q1_b, L0_gnn_k1_w, L0_gnn_k1_b, L0_gnn_v1_w, L0_gnn_v1_b, L0_gnn_s1_w, L0_gnn_s1_b, L0_gnn_q2_w, L0_gnn_q2_b, L0_gnn_k2_w, L0_gnn_k2_b, L0_gnn_v2_w, L0_gnn_v2_b, L0_gnn_s2_w, L0_gnn_s2_b, L0_gnn_lin1_w, L0_gnn_lin1_b, L0_gnn_lin2_w, L0_gnn_lin2_b), axis=-1)
    return x

_drawn_inputs = setup_inputs


def setup_inputs(seed=0):
    import zlib

    import numpy as np

    out = dict(_drawn_inputs(seed))
    spreads = {}
    factors = {'L0_gnn_q1_b': 8.0,
     'L0_gnn_k1_b': 8.0,
     'L0_gnn_q2_w': 2.938,
     'L0_gnn_q2_b': 8.0,
     'L0_gnn_k2_w': 2.939,
     'L0_gnn_k2_b': 8.0}
    for name, (base, spread) in spreads.items():
        noise = np.random.default_rng([zlib.crc32(name.encode()), seed]).standard_normal(out[name].shape)
        drawn = base * np.exp(spread * noise) if base else spread * noise
        out[name] = jnp.asarray(drawn.astype(out[name].dtype))
    for name, factor in factors.items():
        out[name] = (out[name] * factor).astype(out[name].dtype)
    return out
```

```python
import concourse.bass as bass
import numpy as np
from concourse import mybir
from concourse.alu_op_type import AluOpType as ALU
from contextlib import ExitStack

P = 128
NODES, EDGES, F, HEADS = 3125, 50000, 128, 2
CHUNKS = -(-EDGES // P)
BINS = -(-NODES // P)
SLOTS = BINS * P
PAD_NODE = SLOTS - 1
FULL = EDGES // P
TAIL = EDGES - FULL * P
CT = -(-CHUNKS // P)
BLK = 52
NBLK = 8
STEPS = BLK * NBLK
UN = 4
IT = BLK // UN
G = 4
C1 = F + 1
CW = HEADS * C1
BIG = 1e30
EPS_LN = 1e-5
assert CHUNKS + BINS - 1 <= STEPS and BLK % UN == 0


def program(nc, A, out):
    f32, i32, bf16 = mybir.dt.float32, mybir.dt.int32, mybir.dt.bfloat16
    ACT = mybir.ActivationFunctionType
    AX = mybir.AxisListType.X
    x_d, src_d, dst_d = A["x"], A["src"], A["dst"]
    h_d = nc.dram_tensor("h_rows", (SLOTS, F), f32, kind="Internal").ap()
    dl_d = nc.dram_tensor("local_dst_rows", (STEPS, P), bf16, kind="Internal").ap()

    ctx = ExitStack()
    with ctx:
        def sb(name, shape, dt=f32):
            return ctx.enter_context(nc.sbuf_tensor(name, shape, dt))

        def pb(name):
            return ctx.enter_context(nc.psum_tensor(name, [P, 512], f32))

        def sem(name):
            return ctx.enter_context(nc.semaphore(name))

        x_rows = sb("x_rows", [P, BINS, F])
        xT = sb("xT", [P, SLOTS])
        gathered = sb("gathered", [P, 2 * BLK, C1])
        scratch = gathered[:, :, :].rearrange("p s c -> p (s c)")
        used = [0]

        def tmp(shape, dt=f32):
            n = int(np.prod(shape))
            w = n // 2 if dt == bf16 else n
            v = scratch[:, used[0]:used[0] + w]
            used[0] += w
            v = v if dt == f32 else v.bitcast(dt)
            return v if len(shape) == 1 else v.rearrange("p (a b) -> p a b", a=shape[0])
        table = sb("table", [P, BINS, 3, CW], bf16)
        acc = sb("acc", [P, BINS, CW])
        src_i = tmp([CT, P], i32)
        dst_i = tmp([CT, P], i32)
        prev_i = sb("prev_i", [P, CT], i32)
        lastbin_i = sb("lastbin_i", [P, CT], i32)
        prevbin_i = sb("prevbin_i", [P, CT], i32)
        src_f = tmp([CT, P])
        dst_f = tmp([CT, P])
        ends = sb("ends", [P, CT, 4])
        chunk_i = sb("chunk_i", [P, CT], i32)
        chunk_f = sb("chunk_f", [P, CT])
        chunk128 = sb("chunk128", [P, CT])
        key = sb("key", [P, CT])
        keyprev = sb("keyprev", [P, CT])
        step_i = tmp([STEPS], i32)
        step_f = tmp([STEPS])
        step128 = tmp([STEPS])
        rowstep_i = sb("rowstep_i", [P, NBLK], i32)
        rowstep128 = sb("rowstep128", [P, NBLK])
        before = tmp([CT, STEPS])
        sel = tmp([CT, STEPS])
        src_e = sb("src_e", [P, STEPS], i32)
        src_blk = sb("src_blk", [P, 2, BLK], i32)
        dl_e = sb("dl_e", [P, STEPS])
        dl_r = tmp([NBLK, P])[0:BLK]
        dl_rb = tmp([NBLK, P], bf16)[0:BLK]
        bin_f = sb("bin_f", [1, STEPS])
        bin_i = sb("bin_i", [1, STEPS], i32)
        firsts = tmp([STEPS])[0:2]
        lasts = tmp([STEPS])[0:2]
        link = sb("link", [2, STEPS + 1])
        linkneg = sb("linkneg", [2, STEPS + 1])
        single = tmp([STEPS])[0:2]
        carry_f = sb("carry_f", [2, STEPS])
        carry_b = sb("carry_b", [2, NBLK, BLK])
        joined = tmp([STEPS])[0:2]
        seg_f = sb("seg_f", [BLK, NBLK, P], bf16)
        seg_b = sb("seg_b", [BLK, NBLK, P], bf16)
        same = tmp([NBLK, P], bf16)[0:BLK]
        in_last = sb("in_last", [BLK, NBLK, P], bf16)
        in_first = sb("in_first", [BLK, NBLK, P], bf16)
        first_b = sb("first_b", [P, NBLK], bf16)
        first_hot = sb("first_hot", [P, NBLK])
        ident = sb("ident", [P, P])
        ones = sb("ones", [2, P])
        col_i = tmp([P], i32)
        col_b = sb("col_b", [P, P], bf16)
        part_i = sb("part_i", [P, 1], i32)
        part_f = sb("part_f", [P, 1])
        wq = tmp([2, HEADS * F])
        wk = tmp([2, HEADS * F])
        wv = sb("wv", [P, 2, HEADS * F])
        ws = sb("ws", [P, 2, F])
        wl = sb("wl", [P, 2, F])
        wskip = sb("wskip", [P, 2, F])
        bq = sb("bq", [P, 2, HEADS])
        bk = sb("bk", [P, 2, HEADS])
        bv = sb("bv", [HEADS, 2, F])
        bs = sb("bs", [P, 2])
        bl = sb("bl", [P, 2])
        bskip = sb("bskip", [P, 2])
        wqT = tmp([4, F])
        wkT = tmp([4, C1])
        qk = sb("qk", [P, 2, CW])
        qkb = sb("qkb", [1, 2, CW])
        dl_bc = sb("dl_bc", [P, 2, UN * P], bf16)
        hot_t = sb("hot_t", [P, UN, P], bf16)
        hot_e = sb("hot_e", [P, UN, P], bf16)
        whot = sb("whot", [P, UN, HEADS, P])
        junk = sb("junk", [P, UN, HEADS, C1])
        alpha = sb("alpha", [P, HEADS, BLK])
        weight = sb("weight", [P, HEADS, BLK])
        a_row = sb("a_row", [BLK, HEADS, P])
        a_end = sb("a_end", [BLK, 4, P])
        m_end = sb("m_end", [BLK, 4])
        run_f = sb("run_f", [2, BLK + 1])
        run_b = sb("run_b", [2, BLK + 1])
        link_m = sb("link_m", [2, 2, BLK])
        link_c = sb("link_c", [BLK, 4])
        max_f = sb("max_f", [BLK, HEADS, P])
        max_b = sb("max_b", [BLK, HEADS, P])
        max_s = sb("max_s", [BLK, HEADS, P])
        a_off = sb("a_off", [BLK, HEADS, P])
        w_row = sb("w_row", [BLK, HEADS, P])
        drop = sb("drop", [2, 2])
        shrink = sb("shrink", [2, 1])
        shrink_d = sb("shrink_d", [2, 2])
        shrink_1 = sb("shrink_1", [P, 2])
        factor = sb("factor", [P, 2])
        den = sb("den", [P, G * HEADS])
        rden = sb("rden", [P, G * HEADS])
        u_n = sb("u_n", [P, G * HEADS, C1])
        uT = whot[:, :, :, :].rearrange("p (h k) g e -> p h (k g e)", h=HEADS)
        ratio = sb("ratio", [2, G * P])
        hT = sb("hT", [P, G * P])
        h_out = sb("h_out", [P, G, F])
        xin = h_out
        rest = junk[:, :, :, :].rearrange("p k h c -> p k (h c)")
        stats = sb("stats", [P, BINS, 6])
        mv = sb("mv", [P, BINS, 2])
        vare = sb("vare", [P, BINS])
        std = sb("std", [P, BINS])
        rstd = sb("rstd", [P, BINS])
        y_rows = acc[:, :, 0:F]

        ps_t = [pb("ps_t0"), pb("ps_t1")]
        ps_u = [pb("ps_u0"), pb("ps_u1")]
        ps_s = pb("ps_s")
        ps_r = pb("ps_r")
        ps_n = [pb("ps_n0"), pb("ps_n1")]

        pads_set = sem("pads_set")
        consts_set = sem("consts_set")
        edges_in = sem("edges_in")
        x_in = sem("x_in")
        weights_in = sem("weights_in")
        dve_step = sem("dve_step")
        ident_ready = sem("ident_ready")
        sel_ready = sem("sel_ready")
        prep_mm = sem("prep_mm")
        prep_copied = sem("prep_copied")
        rows_ready = sem("rows_ready")
        rows_out = sem("rows_out")
        first_in = sem("first_in")
        skip_ready = sem("skip_ready")
        w_tp = sem("w_tp")
        w_tp_copied = sem("w_tp_copied")
        wk_bias = sem("wk_bias")
        qk_mm = sem("qk_mm")
        qk_ready = sem("qk_ready")
        masks_ready = sem("masks_ready")
        ones_set = sem("ones_set")
        idx_ready = sem("idx_ready")
        got = [sem(f"got{k}") for k in range(UN)]
        dl_in = sem("dl_in")
        hot_t_ready = sem("hot_t_ready")
        t_ready = sem("t_ready")
        alpha_ready = sem("alpha_ready")
        hot_e_ready = sem("hot_e_ready")
        whot_ready = sem("whot_ready")
        u_ready = sem("u_ready")
        u_added = sem("u_added")
        row_tp = sem("row_tp")
        row_ready = sem("row_ready")
        m_end_ready = sem("m_end_ready")
        m_end_tp = sem("m_end_tp")
        link_m_ready = sem("link_m_ready")
        link_tp = sem("link_tp")
        drop_ready = sem("drop_ready")
        shrink_ready = sem("shrink_ready")
        shrink_d_ready = sem("shrink_d_ready")
        factor_mm = sem("factor_mm")
        off_ready = sem("off_ready")
        w_row_ready = sem("w_row_ready")
        w_row_tp = sem("w_row_tp")
        weight_ready = sem("weight_ready")
        scan_step = sem("scan_step")
        xin_ready = sem("xin_ready")
        x_tp = sem("x_tp")
        un_ready = sem("un_ready")
        node_step = sem("node_step")
        uT_tp = sem("uT_tp")
        uT_act = sem("uT_act")
        uT_dve = sem("uT_dve")
        projected = sem("projected")
        hT_ready = sem("hT_ready")
        hT_kept = sem("hT_kept")
        back_tp = sem("back_tp")
        back_free = sem("back_free")
        h_saved = sem("h_saved")
        t_mm = sem("t_mm")
        part1 = sem("part1")
        rest_ready = sem("rest_ready")
        part2 = sem("part2")
        part3 = sem("part3")
        acc_clear = sem("acc_clear")
        var_ready = sem("var_ready")
        std_ready = sem("std_ready")
        y_ready = sem("y_ready")
        y_out = sem("y_out")

        block = ctx.enter_context(nc.Block())
        FG = BINS // G
        REST = BINS - FG * G
        NGR = FG + 1
        N_EDGE_DMA = 6 + CT
        N_WEIGHT_DMA = 20
        PREP = 7
        NAMES = [("q1", "q2"), ("k1", "k2"), ("v1", "v2"), ("s1", "s2"), ("lin1", "lin2")]
        SCAN_LINKS = 10

        def chain(eng, s, base=0):
            n = [0]

            def link_(ins):
                n[0] += 1
                ins.then_inc(s, 1)
                eng.wait_ge(s, base + n[0])
            link_.n = n
            return link_

        def dyn(t, i):
            return t[:, bass.ds(i, 1)]

        def wait_apart(eng, passed, *waits):
            for _, value in waits:
                if not isinstance(value, int):
                    eng.compute_val(value)
            eng.wait_ge(passed, 1)
            for s, value in waits:
                eng.wait_ge(s, value)

        def rev(t):
            return t[:, ::-1]

        def bins_of(eng, etype, step):
            _, v = nc.values_load_multi_w_load_instructions(
                bin_i[0:1, bass.ds(step, UN)], engines=[etype], min_val=0, max_val=BINS - 1,
                skip_runtime_bounds_check_because="a step's bin is step - chunk, within 0..24 by the staircase")
            return v

        @block.sync
        def _(sp):
            sp.wait_ge(pads_set, 4)
            three = (CT - 1) * P
            for d, t in ((dst_d, dst_i), (src_d, src_i)):
                sp.dma_start(t[:, 0:CT - 1, :],
                             d[0:three * P].rearrange("(t p e) -> p t e", p=P, e=P)).then_inc(edges_in, 16)
                sp.dma_start(t[0:FULL - three, CT - 1, :],
                             d[three * P:FULL * P].rearrange("(p e) -> p e", e=P)).then_inc(edges_in, 16)
                sp.dma_start(t[FULL - three:FULL - three + 1, CT - 1, 0:TAIL],
                             d[FULL * P:EDGES].rearrange("(p e) -> p e", p=1)).then_inc(edges_in, 16)
            with nc.allow_non_contiguous_dma(reason="one value of each chunk"):
                lastcol = dst_d[0:FULL * P].rearrange("(c e) -> c e", e=P)[:, P - 1:P]
                sp.dma_start(prev_i[1:P, 0:1], lastcol[0:P - 1, :]).then_inc(edges_in, 16)
                for t in range(1, CT):
                    n = min(P, CHUNKS - t * P)
                    sp.dma_start(prev_i[0:n, t:t + 1],
                                 lastcol[t * P - 1:t * P - 1 + n, :]).then_inc(edges_in, 16)
            sp.dma_start(x_rows[:, 0:BINS - 1, :],
                         x_d[0:(BINS - 1) * P, :].rearrange("(t p) f -> p t f", p=P)).then_inc(x_in, 16)
            sp.dma_start(x_rows[0:NODES - (BINS - 1) * P, BINS - 1, :],
                         x_d[(BINS - 1) * P:NODES, :]).then_inc(x_in, 16)
            sp.wait_ge(rows_ready, 1)
            with nc.allow_non_contiguous_dma(reason="rows of 256 bytes"):
                sp.dma_start(dl_d.rearrange("(j r) e -> r j e", r=BLK), dl_rb[:, :, :]).then_inc(rows_out, 16)
                sp.wait_ge(rows_out, 16)
                sp.dma_start(first_b[:, :],
                             dl_d.rearrange("(j r) e -> j (r e)", r=BLK)[:, 0:1].rearrange("j o -> o j")
                             .to_broadcast([P, NBLK])).then_inc(first_in, 16)
            dl_flat = dl_d.rearrange("(o s) e -> o (s e)", o=1)

            def broadcast(n, g):
                sp.wait_ge(dl_in, 16 * n)
                sp.wait_ge(hot_t_ready, n)
                sp.dma_start(dyn(dl_bc, n % 2).rearrange("p o e -> p (o e)"),
                             dl_flat[:, bass.ds(g * (UN * P), UN * P)].to_broadcast([P, UN * P])
                             ).then_inc(dl_in, 16)
            with sp.Fori(0, STEPS // UN) as g:
                broadcast(g, g)
            broadcast(STEPS // UN, 0)

            def save_h(g, k):
                sp.wait_ge(back_free, g + 1)
                sp.dma_start(h_d.rearrange("(t p) f -> p t f", p=P)[:, bass.ds(g * G, k), :],
                             h_out[:, 0:k, :]).then_inc(h_saved, 16)
                wait_apart(sp, rows_ready, (h_saved, 16 * (g + 1)))
            with sp.Fori(0, FG) as g:
                save_h(g, G)
            save_h(FG, REST)
            with sp.Fori(1, STEPS // UN) as g:
                broadcast(STEPS // UN + g, g)
            broadcast(2 * (STEPS // UN), 0)
            sp.wait_ge(y_ready, BINS)
            sp.dma_start(out[0:(BINS - 1) * P, :].rearrange("(t p) f -> p t f", p=P),
                         y_rows[:, 0:BINS - 1, :]).then_inc(y_out, 16)
            sp.dma_start(out[(BINS - 1) * P:NODES, :],
                         y_rows[0:NODES - (BINS - 1) * P, BINS - 1, :]).then_inc(y_out, 16)
            sp.wait_ge(y_out, 32)

        @block.gpsimd
        def _(pool):
            nc.gpsimd.memset(dst_i[:, :, :], PAD_NODE).then_inc(pads_set, 1)
            nc.gpsimd.memset(src_i[:, :, :], 0).then_inc(pads_set, 1)
            nc.gpsimd.memset(prev_i[:, 0:1], 0)
            nc.gpsimd.memset(prev_i[:, 1:CT], PAD_NODE).then_inc(pads_set, 1)
            nc.gpsimd.memset(x_rows[:, BINS - 1, :], 0.0).then_inc(pads_set, 1)
            nc.gpsimd.iota(chunk_i[:], [[P, CT]], base=0, channel_multiplier=1)
            nc.gpsimd.iota(step_i[:, :], [[1, STEPS]], base=0, channel_multiplier=0)
            nc.gpsimd.iota(rowstep_i[:], [[BLK, NBLK]], base=0, channel_multiplier=1)
            nc.gpsimd.iota(col_i[:, :], [[1, P]], base=0, channel_multiplier=0)
            nc.gpsimd.iota(part_i[:], [[0, 1]], base=0, channel_multiplier=1).then_inc(consts_set, 1)
            nc.gpsimd.memset(acc[:], 0.0).then_inc(acc_clear, 1)
            pool.wait_ge(x_in, 32)

            def feed(g, k):
                pool.wait_ge(x_tp, g)
                nc.gpsimd.tensor_copy(xin[:, 0:k, :], x_rows[:, bass.ds(g * G, k), :]).then_inc(xin_ready, 1)
                pool.wait_ge(hT_ready, g + 1)
                nc.gpsimd.tensor_copy(xT[:, bass.ds(g * G * P, k * P)], hT[:, 0:k * P]).then_inc(hT_kept, 1)
            with pool.Fori(0, FG) as g:
                feed(g, G)
            feed(FG, REST)
            pool.wait_ge(prep_copied, PREP)
            pool.wait_ge(qk_ready, 4)
            pool.wait_ge(masks_ready, 1)
            nc.gpsimd.memset(gathered[:, :, F:C1], 1.0).then_inc(ones_set, 1)

            def gathers(l, rows, s, slots_used):
                for par in range(2):
                    j = s * 2 + par
                    it0 = l * (STEPS // UN) + j * IT
                    if slots_used:
                        for k in range(UN):
                            pool.wait_ge(got[k], 16 * (it0 - IT))
                    nc.gpsimd.tensor_copy(src_blk[:, par, :],
                                          src_e[:, bass.ds(j * BLK, BLK)]).then_inc(idx_ready, 1)
                    pool.wait_ge(idx_ready, l * NBLK + j + 1)
                    for i in range(IT):
                        before_this = 16 * (it0 + i)
                        for k in range(UN):
                            col = i * UN + k
                            waits = [(got[k], before_this)]
                            if slots_used:
                                waits.append((u_ready, l * STEPS + j * BLK + (col + 1 - 2 * BLK)))
                            wait_apart(pool, consts_set, *waits)
                            nc.gpsimd.indirect_dma_start(
                                out=gathered[:, par * BLK + col, 0:F], out_offset=None, in_=rows,
                                in_offset=bass.IndirectOffsetOnAxis(ap=src_blk[:, par, col:col + 1], axis=0),
                            ).then_inc(got[k], 16)
            gathers(0, x_d[:, :], 0, False)
            with pool.Fori(1, NBLK // 2) as s:
                gathers(0, x_d[:, :], s, True)

            def keep(g, k):
                pool.wait_ge(hT_ready, NGR + g + 1)
                nc.gpsimd.tensor_copy(xT[:, bass.ds(g * G * P, k * P)], hT[:, 0:k * P]).then_inc(hT_kept, 1)
            with pool.Fori(0, FG) as g:
                keep(g, G)
            keep(FG, REST)
            pool.wait_ge(un_ready, NGR)
            nc.gpsimd.memset(acc[:], 0.0).then_inc(acc_clear, 1)
            pool.wait_ge(h_saved, 16 * NGR)
            with pool.Fori(0, NBLK // 2) as s:
                gathers(1, h_d[:, :], s, True)

        @block.scalar
        def _(act):
            for l in range(2):
                for n, t in enumerate((wq, wk, wv, ws, wl)):
                    act.dma_start(t[:, l, :], A[f"L0_gnn_{NAMES[n][l]}_w"][:, :]).then_inc(weights_in, 16)
            with nc.allow_non_contiguous_dma(reason="biases as columns"):
                for l in range(2):
                    for n, t in enumerate((bq, bk)):
                        act.dma_start(t[:, l, :], A[f"L0_gnn_{NAMES[n][l]}_b"].rearrange("(h k) -> k h", h=HEADS)
                                      ).then_inc(weights_in, 16)
                    act.dma_start(bv[:, l, :], A[f"L0_gnn_{NAMES[2][l]}_b"].rearrange("(h k) -> h k", h=HEADS)
                                  ).then_inc(weights_in, 16)
                    for n, t in ((3, bs), (4, bl)):
                        act.dma_start(t[:, l:l + 1], A[f"L0_gnn_{NAMES[n][l]}_b"].rearrange("(k o) -> k o", o=1)
                                      ).then_inc(weights_in, 16)

            for m in range(4):
                act.wait_ge(w_tp, m + 1)
                nc.scalar.copy(wqT[:, m, :], ps_t[m % 2][:, 0:F])
                nc.scalar.copy(wkT[:, m, 0:F], ps_t[m % 2][:, F:2 * F]).then_inc(w_tp_copied, 1)
            for m in range(4):
                l, h = divmod(m, 2)
                act.wait_ge(qk_mm, m + 1)
                nc.scalar.mul(qk[:, l, h * C1:(h + 1) * C1], ps_u[m % 2][:, 0:C1], F ** -0.5)
                nc.scalar.mul(qkb[0:1, l, h * C1:(h + 1) * C1], ps_u[m % 2][0:1, 256:256 + C1],
                              F ** -0.5).then_inc(qk_ready, 1)

            def split(z, g, k):
                for t in range(k):
                    T = z * BINS + g * G + t
                    act.wait_ge(t_mm, T + 1)
                    nc.scalar.copy(dyn(table, g * G + t)[:, 0, 0, :], ps_n[t % 2][:, 0:CW]).then_inc(part1, 1)
                    act.wait_ge(rest_ready, T + 1)
                    nc.scalar.copy(dyn(table, g * G + t)[:, 0, 1, :], rest[:, t, :]).then_inc(part2, 1)

            def first_t(g, k):
                act.wait_ge(x_tp, g + 1)
                act.wait_ge(hT_kept, g)
                nc.scalar.copy(hT[:, 0:k * P], ps_u[0][:, 0:k * P]).then_inc(hT_ready, 1)
                split(0, g, k)
            with act.Fori(0, FG) as g:
                first_t(g, G)
            first_t(FG, REST)

            def scan(s):
                act.wait_ge(row_tp, s + 1)
                nc.scalar.copy(a_row[:, :, :].rearrange("p h e -> p (h e)"),
                               ps_s[0:BLK, 0:2 * P]).then_inc(row_ready, 1)
                act.wait_ge(drop_ready, s + 1)
                nc.scalar.activation(shrink[:, :], drop[:, 1:2], ACT.Exp, scale=-1.0).then_inc(shrink_ready, 1)
                act.wait_ge(off_ready, s + 1)
                nc.scalar.activation(w_row[:, :, :], a_off[:, :, :], ACT.Exp).then_inc(w_row_ready, 1)
                act.wait_ge(w_row_tp, s + 1)
                nc.scalar.copy(weight[:, :, :].rearrange("p h e -> p (h e)"),
                               ps_s[:, 256:256 + 2 * BLK]).then_inc(weight_ready, 1)
                act.wait_ge(weight_ready, s + 1)

            def weigh(l, j):
                with act.Fori(0, IT) as i:
                    for k in range(UN):
                        act.wait_ge(hot_e_ready, l * STEPS + j * BLK + i * UN + k + 1)
                        for h in range(HEADS):
                            last = nc.scalar.activation(whot[:, k, h, :], hot_e[:, k, :], ACT.Copy,
                                                        scale=weight[:, h, bass.ds(i * UN + k, 1)])
                        last.then_inc(whot_ready, 1)

            def node(z, g, k):
                m, n = (z - 1) * NGR + g, z * NGR + g
                act.wait_ge(uT_tp, m + 1)
                nc.scalar.copy(uT[:, 0, 0:k * P], ps_t[0][:, 0:k * P])
                nc.scalar.copy(ratio[:, 0:k * P], ps_r[0:2, 0:k * P]).then_inc(uT_act, 1)
                act.wait_ge(projected, m + 1)
                if z == 1:
                    act.wait_ge(hT_kept, n)
                nc.scalar.activation(hT[:, 0:k * P], ps_u[0][:, 0:k * P], ACT.Identity,
                                     bias=bskip[:, z - 1:z]).then_inc(hT_ready, 1)
                if z == 1:
                    split(1, g, k)

            for l in range(2):
                with act.Fori(0, NBLK) as j:
                    scan(l * NBLK + j)
                    weigh(l, j)
                with act.Fori(0, FG) as g:
                    node(l + 1, g, G)
                node(l + 1, FG, REST)
            act.wait_ge(var_ready, 1)
            nc.scalar.activation(std[:, :], vare[:, :], ACT.Sqrt).then_inc(std_ready, 1)

        @block.tensor
        def _(pe):
            PE = mybir.EngineType.PE
            pe.wait_ge(ident_ready, 1)
            pe.wait_ge(weights_in, 16 * N_WEIGHT_DMA)
            for m in range(4):
                l, h = divmod(m, 2)
                if m >= 2:
                    pe.wait_ge(w_tp_copied, m - 1)
                nc.tensor.transpose(ps_t[m % 2][:, 0:F], wq[:, l, h * F:(h + 1) * F], ident[:, :])
                nc.tensor.transpose(ps_t[m % 2][:, F:2 * F], wk[:, l, h * F:(h + 1) * F],
                                    ident[:, :]).then_inc(w_tp, 1)
            pe.wait_ge(wk_bias, 1)
            for m in range(4):
                l, h = divmod(m, 2)
                pe.wait_ge(w_tp_copied, m + 1)
                if m >= 2:
                    pe.wait_ge(qk_ready, m - 1)
                nc.tensor.matmul(ps_u[m % 2][:, 0:C1], wqT[:, m, :], wkT[:, m, :], start=True, stop=True)
                nc.tensor.matmul(ps_u[m % 2][0:1, 256:256 + C1], bq[:, l, h:h + 1], wkT[:, m, :],
                                 start=True, stop=True).then_inc(qk_mm, 1)

            pe.wait_ge(sel_ready, 1)
            banks = [ps_s, ps_r, ps_n[0], ps_n[1]]
            what = [(src_f, None), (dst_f, None), (chunk_f, 1), (ends, 0), (ends, 2)]
            for r in range(PREP):
                if r >= 4:
                    pe.wait_ge(prep_copied, r - 3)
                b = banks[r % 4]
                if r < 5:
                    src, c = what[r]
                    for t in range(CT):
                        lhsT = src[:, t:t + 1] if r == 2 else src[:, t, :] if c is None else src[:, t, c:c + 2]
                        rows = 1 if r == 2 else P if c is None else 2
                        last = nc.tensor.matmul(b[0:rows, 0:STEPS], lhsT, sel[:, t, :],
                                                start=(t == 0), stop=(t == CT - 1))
                else:
                    for j in range(4 * (r - 5), 4 * (r - 5) + 4):
                        for t in range(CT):
                            last = nc.tensor.matmul(b[0:BLK, (j % 4) * P:(j % 4 + 1) * P],
                                                    sel[:, t, j * BLK:(j + 1) * BLK], dst_f[:, t, :],
                                                    start=(t == 0), stop=(t == CT - 1))
                last.then_inc(prep_mm, 1)
            pe.wait_ge(prep_copied, PREP)
            pe.wait_ge(qk_ready, 4)

            def make_t(z, g, k):
                for t in range(k):
                    T = z * BINS + g * G + t
                    pe.wait_ge(rest_ready, T if t == 0 else T - 1)
                    nc.tensor.matmul(ps_n[t % 2][:, 0:CW], hT[:, t * P:(t + 1) * P], qk[:, z, :],
                                     start=True, stop=False)
                    nc.tensor.matmul(ps_n[t % 2][:, 0:CW], ones[0:1, :], qkb[0:1, z, :],
                                     start=False, stop=True).then_inc(t_mm, 1)

            def first_t(g, k):
                pe.wait_ge(xin_ready, g + 1)
                for t in range(k):
                    last = nc.tensor.transpose(ps_u[0][:, t * P:(t + 1) * P], xin[:, t, :], ident[:, :])
                last.then_inc(x_tp, 1)
                pe.wait_ge(hT_ready, g + 1)
                make_t(0, g, k)
            with pe.Fori(0, FG) as g:
                first_t(g, G)
            first_t(FG, REST)

            def step_t(b, a, k):
                pe.wait_ge(alpha_ready, a + 1)
                for part in range(3):
                    last = nc.tensor.matmul(ps_t[k % 2][:, 0:CW], hot_t[:, k, :],
                                            dyn(table, b[k])[:, 0, part, :], start=(part == 0), stop=(part == 2))
                last.then_inc(t_ready, 1)

            def step_u(slot, c, k):
                pe.wait_ge(whot_ready, c + 1)
                pe.wait_ge(u_added, c + 1)
                for h in range(HEADS):
                    last = nc.tensor.matmul(ps_u[k % 2][:, h * C1:(h + 1) * C1], whot[:, k, h, :],
                                            dyn(gathered, slot + k)[:, 0, :], start=True, stop=True)
                last.then_inc(u_ready, 1)

            def blocks(l, ja, jc):
                with pe.Fori(0, IT) as i:
                    if ja is not None:
                        b = bins_of(pe, PE, ja * BLK + i * UN)
                        a = l * STEPS + ja * BLK + i * UN
                        pe.wait_ge(hot_t_ready, l * (STEPS // UN) + ja * IT + i + 1)
                    if jc is not None:
                        c = l * STEPS + jc * BLK + i * UN
                        slot = (jc % 2) * BLK + i * UN
                    if jc is None:
                        for k in range(UN):
                            step_t(b, a + k, k)
                    elif ja is None:
                        for k in range(UN):
                            step_u(slot, c + k, k)
                    else:
                        step_t(b, a, 0)
                        for k in range(1, UN):
                            step_t(b, a + k, k)
                            step_u(slot, c + k - 1, k - 1)
                        step_u(slot, c + UN - 1, UN - 1)

            def scan(s):
                wait_apart(pe, ident_ready, (alpha_ready, 2 + (s + 1) * BLK))
                for h in range(HEADS):
                    last = nc.tensor.transpose(ps_s[0:BLK, h * P:(h + 1) * P], alpha[:, h, :], ident[:, :])
                last.then_inc(row_tp, 1)
                wait_apart(pe, ident_ready, (m_end_ready, s + 1))
                for n in range(2):
                    last = nc.tensor.transpose(ps_r[0:2, n * 64:n * 64 + BLK], m_end[:, 2 * n:2 * n + 2],
                                               ident[0:BLK, 0:BLK])
                last.then_inc(m_end_tp, 1)
                wait_apart(pe, ident_ready, (link_m_ready, s + 1))
                for n in range(2):
                    last = nc.tensor.transpose(ps_r[0:BLK, 256 + 2 * n:258 + 2 * n], link_m[:, n, :],
                                               ident[0:2, 0:2])
                last.then_inc(link_tp, 1)
                wait_apart(pe, ident_ready, (shrink_d_ready, s + 1))
                nc.tensor.matmul(ps_r[:, 300:302], ones[:, :], shrink_d[:, :],
                                 start=True, stop=True).then_inc(factor_mm, 1)
                wait_apart(pe, ident_ready, (w_row_ready, s + 1))
                for h in range(HEADS):
                    last = nc.tensor.transpose(ps_s[:, 256 + h * BLK:256 + (h + 1) * BLK], w_row[:, h, :],
                                               ident[0:BLK, 0:BLK])
                last.then_inc(w_row_tp, 1)

            def node(z, g, k):
                m, n = (z - 1) * NGR + g, z * NGR + g
                pe.wait_ge(un_ready, m + 1)
                for t in range(k):
                    for h in range(HEADS):
                        nc.tensor.transpose(ps_t[h][:, t * P:(t + 1) * P], u_n[:, t * HEADS + h, 0:F], ident[:, :])
                    last = nc.tensor.transpose(ps_r[0:2, t * P:(t + 1) * P],
                                               u_n[:, t * HEADS:(t + 1) * HEADS, F], ident[:, :])
                last.then_inc(uT_tp, 1)
                pe.wait_ge(uT_act, m + 1)
                pe.wait_ge(uT_dve, m + 1)
                w = k * P
                for h in range(HEADS):
                    nc.tensor.matmul(ps_u[0][:, 0:w], wv[:, z - 1, h * F:(h + 1) * F], uT[:, h, 0:w],
                                     start=(h == 0), stop=False)
                nc.tensor.matmul(ps_u[0][:, 0:w], bv[:, z - 1, :], ratio[:, 0:w], start=False, stop=False)
                nc.tensor.matmul(ps_u[0][:, 0:w], wskip[:, z - 1, :], xT[:, bass.ds(g * G * P, w)],
                                 start=False, stop=True).then_inc(projected, 1)
                pe.wait_ge(hT_ready, n + 1)
                pe.wait_ge(back_free, m)
                for t in range(k):
                    last = nc.tensor.transpose(ps_u[1][:, t * P:(t + 1) * P], hT[:, t * P:(t + 1) * P], ident[:, :])
                last.then_inc(back_tp, 1)
                if z == 1:
                    make_t(1, g, k)

            for l in range(2):
                pe.wait_ge(part3, (l + 1) * BINS)
                blocks(l, 0, None)
                with pe.Fori(0, NBLK - 1) as j:
                    scan(l * NBLK + j)
                    blocks(l, j + 1, j)
                scan(l * NBLK + NBLK - 1)
                blocks(l, None, NBLK - 1)
                with pe.Fori(0, FG) as g:
                    node(l + 1, g, G)
                node(l + 1, FG, REST)

        @block.vector
        def _(dve):
            DVE = mybir.EngineType.DVE
            V = nc.vector
            step = chain(dve, dve_step)
            dve.wait_ge(consts_set, 1)
            V.tensor_copy(col_b[:, :], col_i[:, :])
            step(V.tensor_copy(part_f[:, :], part_i[:, :]))
            V.memset(ones[:, :], 1.0)
            V.memset(run_b[:, :], -BIG)
            V.memset(link[:, :], 0.0).then_inc(alpha_ready, 2)
            V.memset(seg_f[:, :, 0:1], 0.0).then_inc(u_added, 2)
            V.memset(seg_b[:, :, 0:1], 0.0)
            V.tensor_scalar(ident[:, :], col_b[:, :], part_f[:, 0:1], None, ALU.is_equal).then_inc(ident_ready, 1)

            V.tensor_copy(chunk_f[:, :], chunk_i[:, :])
            V.tensor_copy(step_f[:, :], step_i[:, :])
            V.tensor_scalar(step128[:, :], step_i[:, :], float(P), None, ALU.mult)
            V.tensor_scalar(rowstep128[:, :], rowstep_i[:, :], float(P), None, ALU.mult)
            V.tensor_scalar(chunk128[:, :], chunk_i[:, :], float(P), None, ALU.mult)
            dve.wait_ge(edges_in, 16 * N_EDGE_DMA)
            V.tensor_scalar(lastbin_i[:, :], dst_i[:, :, P - 1], 7, None, ALU.arith_shift_right)
            V.tensor_scalar(prevbin_i[:, :], prev_i[:, :], 7, None, ALU.arith_shift_right)
            step(V.tensor_copy(src_f[:, :, :], src_i[:, :, :]))
            V.tensor_tensor(key[:, :], lastbin_i[:, :], chunk_f[:, :], ALU.add)
            V.scalar_tensor_tensor(out=keyprev[:, :], in0=prevbin_i[:, :], scalar=-1.0, in1=chunk_f[:, :],
                                   op0=ALU.add, op1=ALU.add)
            for t in range(CT):
                last = V.tensor_scalar(dst_f[:, t, :], dst_i[:, t, :], chunk128[:, t:t + 1], None, ALU.add)
            step(last)
            for t in range(CT):
                last = V.tensor_scalar(before[:, t, :], step_f[:, :], key[:, t:t + 1], None, ALU.is_le)
            step(last)
            V.tensor_copy(ends[:, :, 0:2], dst_f[:, :, 0:1].to_broadcast([P, CT, 2]))
            V.tensor_copy(ends[:, :, 2:4], dst_f[:, :, P - 1:P].to_broadcast([P, CT, 2]))
            for t in range(CT):
                last = V.scalar_tensor_tensor(out=sel[:, t, :], in0=step_f[:, :], scalar=keyprev[:, t:t + 1],
                                              in1=before[:, t, :], op0=ALU.is_gt, op1=ALU.mult)
            last.then_inc(sel_ready, 1)

            dve.wait_ge(weights_in, 16 * N_WEIGHT_DMA)
            V.tensor_tensor(wskip[:, :, :], ws[:, :, :], wl[:, :, :], ALU.add)
            V.tensor_tensor(bskip[:, :], bs[:, :], bl[:, :], ALU.add)
            V.tensor_copy(wkT[:, :, F], bk[:, :, :].rearrange("p l h -> p (l h)")).then_inc(wk_bias, 1)

            dve.wait_ge(prep_mm, 1)
            V.tensor_copy(src_e[:, :], ps_s[:, 0:STEPS]).then_inc(prep_copied, 1)
            dve.wait_ge(prep_mm, 2)
            V.tensor_tensor(dl_e[:, :], ps_r[:, 0:STEPS], step128[:, :], ALU.subtract).then_inc(prep_copied, 1)
            dve.wait_ge(prep_mm, 3)
            V.tensor_tensor(bin_i[:, :], step_f[0:1, :], ps_n[0][0:1, 0:STEPS], ALU.subtract).then_inc(prep_copied, 1)
            dve.wait_ge(prep_mm, 4)
            V.tensor_tensor(firsts[:, :], ps_n[1][0:2, 0:STEPS], step128[0:2, :], ALU.subtract).then_inc(prep_copied, 1)
            dve.wait_ge(prep_mm, 5)
            V.tensor_tensor(lasts[:, :], ps_s[0:2, 0:STEPS], step128[0:2, :], ALU.subtract).then_inc(prep_copied, 1)
            for r in range(2):
                dve.wait_ge(prep_mm, 6 + r)
                for j in range(4 * r, 4 * r + 4):
                    last = V.tensor_scalar(dl_r[:, j, :], (ps_r, ps_n[0])[r][0:BLK, (j % 4) * P:(j % 4 + 1) * P],
                                           rowstep128[0:BLK, j:j + 1], None, ALU.subtract)
                last.then_inc(prep_copied, 1)
            dve.wait_ge(prep_copied, PREP)
            V.tensor_copy(dl_rb[:, :, :], dl_r[:, :, :]).then_inc(rows_ready, 1)

            def penalty(o, i):
                return V.tensor_scalar(o, i, 1.0, BIG, ALU.subtract, ALU.mult)
            V.tensor_tensor(same[:, :, 0:P - 1], dl_r[:, :, 1:P], dl_r[:, :, 0:P - 1], ALU.is_equal)
            V.tensor_tensor(in_last[:, :, :], dl_r[:, :, :], dl_r[:, :, P - 1:P].to_broadcast([BLK, NBLK, P]),
                            ALU.is_equal)
            V.tensor_tensor(in_first[:, :, :], dl_r[:, :, :], dl_r[:, :, 0:1].to_broadcast([BLK, NBLK, P]),
                            ALU.is_equal)
            V.tensor_tensor(link[:, 1:STEPS], lasts[:, 0:STEPS - 1], firsts[:, 1:STEPS], ALU.is_equal)
            step(V.tensor_tensor(single[:, :], firsts[:, :], lasts[:, :], ALU.is_equal))
            penalty(seg_f[:, :, 1:P], same[:, :, 0:P - 1])
            penalty(seg_b[:, :, 1:P], same[:, :, P - 2::-1])
            penalty(linkneg[:, :], link[:, :])
            V.tensor_tensor(carry_f[:, :], link[:, 0:STEPS], single[:, :], ALU.mult)
            step(V.tensor_tensor(joined[:, :], link[:, 1:STEPS + 1], single[:, :], ALU.mult))
            penalty(in_last[:, :, :], in_last[:, :, :])
            penalty(in_first[:, :, :], in_first[:, :, :])
            penalty(carry_f[:, :], carry_f[:, :])
            step(penalty(carry_b[:, :, :], joined.rearrange("p (j r) -> p j r", r=BLK)[:, :, ::-1]))
            dve.wait_ge(first_in, 16)
            (V.tensor_scalar(first_hot[:, :], first_b[:, :], part_f[:, 0:1], None,
                             ALU.is_equal)).then_inc(masks_ready, 1)

            def split(z, g, k):
                dve.wait_ge(part3, z * BINS + g * G)
                for t in range(k):
                    dve.wait_ge(part1, z * BINS + g * G + t + 1)
                    V.tensor_tensor(rest[:, t, :], ps_n[t % 2][:, 0:CW], dyn(table, g * G + t)[:, 0, 0, :],
                                    ALU.subtract).then_inc(rest_ready, 1)
                for t in range(k):
                    T = z * BINS + g * G + t
                    dve.wait_ge(part2, T + 1)
                    dve.wait_ge(rest_ready, T + 1)
                    V.tensor_tensor(dyn(table, g * G + t)[:, 0, 2, :], rest[:, t, :],
                                    dyn(table, g * G + t)[:, 0, 1, :], ALU.subtract).then_inc(part3, 1)
            with dve.Fori(0, FG) as g:
                split(0, g, G)
            split(0, FG, REST)

            def one_hot_t(n):
                dve.wait_ge(dl_in, 16 * (n + 1))
                V.tensor_scalar(hot_t[:, :, :].rearrange("p k e -> p (k e)"),
                                dyn(dl_bc, n % 2)[:, 0, :], part_f[:, 0:1], None,
                                ALU.is_equal).then_inc(hot_t_ready, 1)

            def step_alpha(l, j, i, k, slot):
                a = l * STEPS + j * BLK + i * UN + k
                dve.wait_ge(t_ready, a + 1)
                dve.wait_ge(got[k], 16 * (l * (STEPS // UN) + j * IT + i + 1))
                for h in range(HEADS):
                    last = V.scalar_tensor_tensor(
                        out=junk[:, k, h, :], in0=ps_t[k % 2][:, h * C1:(h + 1) * C1], scalar=1.0,
                        in1=dyn(gathered, slot + k)[:, 0, :], op0=ALU.mult, op1=ALU.mult,
                        accum_out=alpha[:, h, bass.ds(i * UN + k, 1)])
                last.then_inc(alpha_ready, 1)

            def step_add(l, j, i, k, b):
                c = l * STEPS + j * BLK + i * UN + k
                dve.wait_ge(u_ready, c + 1)
                dve.wait_ge(u_added, c + 2)
                V.tensor_tensor(dyn(acc, b[k])[:, 0, :], ps_u[k % 2][:, 0:CW], dyn(acc, b[k])[:, 0, :],
                                ALU.add).then_inc(u_added, 1)

            def blocks(l, ja, jc):
                with dve.Fori(0, IT) as i:
                    if jc is not None:
                        b = bins_of(dve, DVE, jc * BLK + i * UN)
                        for k in range(UN):
                            V.tensor_scalar(hot_e[:, k, :], col_b[:, :],
                                            dl_e[:, bass.ds(jc * BLK + i * UN + k, 1)], None,
                                            ALU.is_equal).then_inc(hot_e_ready, 1)
                    if ja is not None:
                        slot = (ja % 2) * BLK + i * UN
                        dve.wait_ge(alpha_ready, 2 + (l * STEPS + ja * BLK + i * UN))
                    for k in range(UN):
                        if ja is not None:
                            step_alpha(l, ja, i, k, slot)
                        if ja is not None and k == UN - 1:
                            one_hot_t(l * (STEPS // UN) + ja * IT + i + 1)
                        if jc is not None and k >= 1:
                            step_add(l, jc, i, k - 1, b)
                    if jc is not None:
                        step_add(l, jc, i, UN - 1, b)

            def scan(l, j):
                s = l * NBLK + j
                ln = chain(dve, scan_step, s * SCAN_LINKS)
                p0 = j * BLK
                dve.wait_ge(row_ready, s + 1)
                two = a_row[:, :, :]
                for n, mask in enumerate((in_last, in_first)):
                    last = V.tensor_tensor(a_end[:, 2 * n:2 * n + 2, :], two,
                                           dyn(mask, j).to_broadcast([BLK, HEADS, P]), ALU.add)
                ln(last)
                V.tensor_reduce(m_end[:, :], a_end[:, :, :], AX, ALU.max).then_inc(m_end_ready, 1)
                dve.wait_ge(m_end_tp, s + 1)
                V.tensor_tensor_scan(run_f[:, 1:BLK + 1], carry_f[:, bass.ds(p0, BLK)], ps_r[0:2, 0:BLK],
                                     run_f[:, 0:1], ALU.add, ALU.max)
                ln(V.tensor_tensor_scan(rev(run_b[:, 0:BLK]),
                                        dyn(carry_b, j)[:, 0, :], rev(ps_r[0:2, 64:64 + BLK]),
                                        -BIG, ALU.add, ALU.max))
                V.tensor_tensor(link_m[:, 0, :], run_f[:, 0:BLK], linkneg[:, bass.ds(p0, BLK)], ALU.add)
                V.tensor_tensor(link_m[:, 1, :], run_b[:, 1:BLK + 1], linkneg[:, bass.ds(p0 + 1, BLK)],
                                ALU.add).then_inc(link_m_ready, 1)
                ln(V.scalar_tensor_tensor(out=drop[:, 0:1], in0=run_b[:, 0:1], scalar=run_f[:, 0:1],
                                          in1=run_f[:, 0:1], op0=ALU.max, op1=ALU.subtract))
                V.tensor_tensor(drop[:, 1:2], drop[:, 0:1], link[:, bass.ds(p0, 1)], ALU.mult).then_inc(drop_ready, 1)
                ln(V.tensor_copy(run_f[:, 0:1], run_f[:, BLK:BLK + 1]))
                dve.wait_ge(link_tp, s + 1)
                ln(V.tensor_copy(link_c[:, :], ps_r[0:BLK, 256:260]))
                for h in range(HEADS):
                    V.tensor_tensor_scan(max_f[:, h, :], dyn(seg_f, j)[:, 0, :], a_row[:, h, :],
                                         link_c[:, h:h + 1], ALU.add, ALU.max)
                    last = V.tensor_tensor_scan(rev(max_b[:, h, :]), dyn(seg_b, j)[:, 0, :], rev(a_row[:, h, :]),
                                                link_c[:, 2 + h:3 + h], ALU.add, ALU.max)
                ln(last)
                ln(V.tensor_tensor(max_s[:, :, :], max_f[:, :, :], max_b[:, :, :], ALU.max))
                V.tensor_tensor(a_off[:, :, :], a_row[:, :, :], max_s[:, :, :], ALU.subtract).then_inc(off_ready, 1)
                dve.wait_ge(shrink_ready, s + 1)
                V.tensor_scalar(shrink_d[:, :], ident[0:2, 0:2], shrink[:, 0:1], None,
                                ALU.mult).then_inc(shrink_d_ready, 1)
                dve.wait_ge(factor_mm, s + 1)
                ln(V.tensor_scalar(shrink_1[:, :], ps_r[:, 300:302], 1.0, None, ALU.subtract))
                ln(V.tensor_scalar(factor[:, :], shrink_1[:, :], first_hot[:, bass.ds(j, 1)], 1.0, ALU.mult, ALU.add))
                dve.wait_ge(u_added, 2 + (l * STEPS + p0))
                b = bins_of(dve, DVE, p0)
                for h in range(HEADS):
                    o = dyn(acc, b[0])[:, 0, h * C1:(h + 1) * C1]
                    last = V.tensor_scalar(o, o, factor[:, h:h + 1], None, ALU.mult)
                last.then_inc(scan_step, 1)
                assert ln.n[0] + 1 == SCAN_LINKS, ln.n[0]
                wait_apart(dve, consts_set, (scan_step, (s + 1) * SCAN_LINKS))

            def node(z, g, k):
                m = (z - 1) * NGR + g
                sums = acc[:, bass.ds(g * G, k), :].rearrange("p t (h c) -> p (t h) c", h=HEADS)
                ln = chain(dve, node_step, 2 * m)
                ln(V.tensor_scalar(den[:, 0:2 * k], sums[:, :, F], 1e-16, float(HEADS), ALU.add, ALU.mult))
                ln(V.reciprocal(rden[:, 0:2 * k], den[:, 0:2 * k]))
                V.tensor_tensor(u_n[:, 0:2 * k, :], sums,
                                rden[:, 0:2 * k].rearrange("p (t o) -> p t o", o=1).to_broadcast([P, 2 * k, C1]),
                                ALU.mult).then_inc(un_ready, 1)
                dve.wait_ge(uT_tp, m + 1)
                V.tensor_copy(uT[:, 1, 0:k * P], ps_t[1][:, 0:k * P]).then_inc(uT_dve, 1)
                dve.wait_ge(back_tp, m + 1)
                if z == 1:
                    dve.wait_ge(h_saved, 16 * g)
                    V.tensor_copy(h_out[:, 0:k, :].rearrange("p t f -> p (t f)"),
                                  ps_u[1][:, 0:k * P]).then_inc(back_free, 1)
                    split(1, g, k)
                else:
                    rows = x_rows[:, bass.ds(g * G, k), :]
                    V.tensor_tensor(rows, rows, ps_u[1][:, 0:k * P].rearrange("p (t f) -> p t f", t=k),
                                    ALU.add).then_inc(back_free, 1)

            dve.wait_ge(ones_set, 1)
            one_hot_t(0)
            for l in range(2):
                dve.wait_ge(acc_clear, l + 1)
                step(V.memset(run_f[:, 0:1], -BIG))
                blocks(l, 0, None)
                with dve.Fori(0, NBLK - 1) as j:
                    scan(l, j)
                    blocks(l, j + 1, j)
                scan(l, NBLK - 1)
                blocks(l, None, NBLK - 1)
                dve.wait_ge(u_added, 2 + (l + 1) * STEPS)
                with dve.Fori(0, FG) as g:
                    node(l + 1, g, G)
                node(l + 1, FG, REST)

            dve.wait_ge(back_free, 2 * NGR)
            for t in range(BINS):
                last = V.bn_stats(stats[:, t, :], x_rows[:, t, :])
            step(last)
            for t in range(BINS):
                last = V.bn_aggr(mv[:, t, :], stats[:, t, :])
            step(last)
            V.tensor_scalar(vare[:, :], mv[:, :, 1], EPS_LN, None, ALU.add).then_inc(var_ready, 1)
            dve.wait_ge(std_ready, 1)
            step(V.reciprocal(rstd[:, :], std[:, :]))
            for t in range(BINS):
                V.tensor_scalar(y_rows[:, t, :], x_rows[:, t, :], mv[:, t, 0:1], rstd[:, t:t + 1],
                                ALU.subtract, ALU.mult).then_inc(y_ready, 1)


_INS = ["x", "src", "dst"] + [f"L0_gnn_{n}_{k}" for n in ("q1", "k1", "v1", "s1", "q2", "k2", "v2", "s2", "lin1", "lin2")
                              for k in ("w", "b")]


def kernel(**inputs):
    import numpy as _np
    import concourse.bacc as _bacc
    from concourse import mybir as _mybir
    from concourse.bass_utils import run_bass_kernel_spmd as _run

    nc = _bacc.Bacc("TRN2", target_bir_lowering=False, num_devices=1)
    arrays, args = {}, {}
    for name in _INS:
        a = _np.ascontiguousarray(inputs[name])
        arrays[f"in_{name}"] = a
        args[name] = nc.dram_tensor(f"in_{name}", a.shape, _mybir.dt.from_np(a.dtype), kind="ExternalInput").ap()
    out = nc.dram_tensor("out", (NODES, F), _mybir.dt.float32, kind="ExternalOutput").ap()
    program(nc, args, out)
    r = _run(nc, [arrays], core_ids=[0])
    return r.results[0]["out"]
```

```python
import concourse.bass as bass
import numpy as np
from concourse import mybir
from concourse.alu_op_type import AluOpType as ALU
from contextlib import ExitStack

P = 128
NODES, EDGES, F, HEADS = 3125, 50000, 128, 2
CHUNKS = -(-EDGES // P)
BINS = -(-NODES // P)
SLOTS = BINS * P
PAD_NODE = SLOTS - 1
FULL = EDGES // P
TAIL = EDGES - FULL * P
CT = -(-CHUNKS // P)
BLK = 52
NBLK = 8
STEPS = BLK * NBLK
RING = 2 * BLK
UN = 4
BC = 8
GQ = 8
S_SLOTS = 10
LAG = BLK + S_SLOTS
NB = 3
G = 4
NGR = -(-BINS // G)
C1 = F + 1
CW = HEADS * C1
BIG = 1e30
EPS_LN = 1e-5
assert CHUNKS + BINS - 1 <= STEPS and BLK % UN == 0 and STEPS % RING == 0 and STEPS % GQ == 0


def group(g):
    k = min(G, BINS - g * G)
    return g * G, k, k * P


def program(nc, A, out):
    f32, i32, bf16 = mybir.dt.float32, mybir.dt.int32, mybir.dt.bfloat16
    ACT = mybir.ActivationFunctionType
    AX = mybir.AxisListType.X
    x_d, src_d, dst_d = A["x"], A["src"], A["dst"]
    h_d = nc.dram_tensor("h_rows", (SLOTS, F), f32, kind="Internal").ap()
    dl_d = nc.dram_tensor("local_dst_rows", (STEPS, P), bf16, kind="Internal").ap()

    ctx = ExitStack()
    with ctx:
        def sb(name, shape, dt=f32):
            return ctx.enter_context(nc.sbuf_tensor(name, shape, dt))

        def sem(name):
            return ctx.enter_context(nc.semaphore(name))

        x_rows = sb("x_rows", [P, BINS, F])
        xT = sb("xT", [P, SLOTS])
        gathered = sb("gathered", [P, RING, C1])
        table = sb("table", [P, BINS, 3, CW], bf16)
        acc = sb("acc", [P, BINS, CW])

        def lender(whole):
            used = [0]

            def lend(shape, dt=f32):
                n = int(np.prod(shape))
                w = n // 2 if dt == bf16 else n
                v = whole[:, used[0]:used[0] + w]
                used[0] += w
                v = v if dt == f32 else v.bitcast(dt)
                if len(shape) == 2:
                    v = v.rearrange("p (a b) -> p a b", a=shape[0])
                if len(shape) == 3:
                    v = v.rearrange("p (a b c) -> p a b c", a=shape[0], b=shape[1])
                return v
            return lend

        tmp = lender(acc[:, :, :].rearrange("p t c -> p (t c)"))
        src_i = tmp([CT, P], i32)
        dst_i = tmp([CT, P], i32)
        src_f = tmp([CT, P])
        dst_f = tmp([CT, P])
        before = tmp([CT, STEPS])
        sel = tmp([CT, STEPS])
        step_f = tmp([STEPS])
        step128 = tmp([STEPS])
        tmp = lender(gathered[:, BLK:RING, :].rearrange("p s c -> p (s c)"))
        wq = tmp([2, HEADS * F])
        wk = tmp([2, HEADS * F])
        wqT = tmp([4, F])
        wkT = tmp([4, C1])
        dl_r = tmp([NBLK, P])[0:BLK]
        dl_rb = tmp([NBLK, P], bf16)[0:BLK]
        same = tmp([NBLK, P], bf16)[0:BLK]
        firsts = tmp([STEPS])[0:2]
        lasts = tmp([STEPS])[0:2]
        single = tmp([STEPS])[0:2]
        joined = tmp([STEPS])[0:2]
        wlin = tmp([2, F])
        bq_wide = tmp([P])
        bs = tmp([2])
        bl = tmp([2])
        tmp = lender(gathered[:, :, :].rearrange("p s c -> p (s c)"))
        u_n = [tmp([G * HEADS, C1]) for _ in range(2)]
        uT = [tmp([HEADS, G * P]) for _ in range(2)]
        ratio = [tmp([G * P])[0:2] for _ in range(2)]
        h_out = [tmp([G, F]) for _ in range(2)]
        den = tmp([NGR, G * HEADS])
        rden = tmp([NGR, G * HEADS])
        stats = tmp([BINS, 6])
        mv = tmp([BINS, 2])
        vare = tmp([BINS])
        std = tmp([BINS])
        rstd = tmp([BINS])

        prev_i = sb("prev_i", [P, CT], i32)
        lastbin_i = sb("lastbin_i", [P, CT], i32)
        prevbin_i = sb("prevbin_i", [P, CT], i32)
        ends = sb("ends", [P, CT, 4])
        chunk_f = sb("chunk_f", [P, CT])
        chunk128 = sb("chunk128", [P, CT])
        key = sb("key", [P, CT])
        keyprev = sb("keyprev", [P, CT])
        rowstep_f = sb("rowstep_f", [P, NBLK])
        rowstep128 = sb("rowstep128", [P, NBLK])
        src_e = sb("src_e", [P, STEPS], i32)
        dl_e = sb("dl_e", [P, STEPS])
        bin_i = sb("bin_i", [1, STEPS], i32)
        link = sb("link", [2, STEPS + 1])
        linkneg = sb("linkneg", [2, STEPS + 1])
        carry_f = sb("carry_f", [2, STEPS])
        carry_b = sb("carry_b", [2, NBLK, BLK])
        seg_f = sb("seg_f", [BLK, NBLK, P], bf16)
        seg_b = sb("seg_b", [BLK, NBLK, P], bf16)
        in_last = sb("in_last", [BLK, NBLK, P], bf16)
        in_first = sb("in_first", [BLK, NBLK, P], bf16)
        first_b = sb("first_b", [P, NBLK], bf16)
        first_hot = sb("first_hot", [P, NBLK])
        ident = sb("ident", [P, P])
        ones = sb("ones", [2, P])
        col_f = sb("col_f", [P, P])
        col_b = sb("col_b", [P, P], bf16)
        part_f = sb("part_f", [P, 1])
        wv = sb("wv", [P, 2, HEADS * F])
        wskip = sb("wskip", [P, 2, F])
        bq = sb("bq", [P, 2, HEADS])
        bk = sb("bk", [P, 2, HEADS])
        bv = sb("bv", [HEADS, 2, F])
        bskip = sb("bskip", [P, 2])
        qk = sb("qk", [P, 2, CW])
        qk_bias = sb("qk_bias", [P, 2, CW])
        dl_bc = sb("dl_bc", [P, 2, BC * P], bf16)
        hot_t = sb("hot_t", [P, 2, UN, P], bf16)
        hot_e = sb("hot_e", [P, UN, P], bf16)
        whot = sb("whot", [P, UN, HEADS, P])
        junk = sb("junk", [P, UN, HEADS, C1])
        alpha = sb("alpha", [P, 2, HEADS, BLK])
        weight = sb("weight", [P, 2, HEADS, BLK])
        a_row = sb("a_row", [BLK, HEADS, P])
        a_end = sb("a_end", [BLK, 4, P])
        m_end = sb("m_end", [BLK, 4])
        run_f = sb("run_f", [2, BLK + 1])
        run_b = sb("run_b", [2, BLK + 1])
        link_m = sb("link_m", [2, 2, BLK])
        link_c = sb("link_c", [BLK, 4])
        max_f = sb("max_f", [BLK, HEADS, P])
        max_b = sb("max_b", [BLK, HEADS, P])
        max_s = sb("max_s", [BLK, HEADS, P])
        a_off = sb("a_off", [BLK, HEADS, P])
        w_row = sb("w_row", [BLK, HEADS, P])
        drop = sb("drop", [2, 2])
        shrink = sb("shrink", [2, 1])
        shrink_d = sb("shrink_d", [2, 2])
        shrink_1 = sb("shrink_1", [P, 2])
        factor = sb("factor", [P, 2])
        rest = sb("rest", [P, G, CW])
        left = sb("left", [P, G, CW])

        ps = ctx.enter_context(nc.psum_tensor("ps", [P, 8, 512], f32))
        bank_t = [ps[:, i, :] for i in (0, 1, 2)]
        bank_u = [ps[:, i, :] for i in (3, 4, 5)]
        bank_s, bank_r = ps[:, 6, :], ps[:, 7, :]
        bank_x = [ps[:, 0, :], ps[:, 1, :]]
        bank_h1 = ps[:, 2, :]
        bank_p = [ps[:, 3, :], ps[:, 4, :]]
        bank_b = ps[:, 5, :]
        bank_w = ps[:, 7, :]
        bank_T = ps[:, 3:7, :]

        SEMS = """pads_set consts_set edges_in x_in weights_in wide_in dve_step ident_ready sel_ready prep_mm
        prep_copied rows_ready rows_out first_in masks_ready ones_set weights_tp weights_tp_copied wk_bias
        bq_ready qk_mm qk_ready hot_t_ready t_ready alpha_ready hot_e_ready whot_ready u_ready u_added
        row_tp row_ready ends_ready m_end_ready m_end_tp link_m_ready link_tp drop_ready shrink_ready
        shrink_d_ready factor_mm off_ready w_row_ready w_row_tp weight_ready scan_step acc_clear
        x_tp xT_ready un_ready node_step uT_tp uT_act uT_dve projected back_tp back_read
        t_mm t_biased part1 left_ready part2 part3 var_ready std_ready y_ready y_out""".split()
        S = {n: sem(n) for n in SEMS}
        got = [sem(f"got{k}") for k in range(GQ)]
        h_saved = [sem(f"h_saved{k}") for k in range(2)]
        dl_in = [sem(f"dl_in{k}") for k in range(2)]

        block = ctx.enter_context(nc.Block())
        N_EDGE_DMA = 6 + CT
        N_WEIGHT_DMA = 20
        PREP = 7
        NAMES = [("q1", "q2"), ("k1", "k2"), ("v1", "v2"), ("s1", "s2"), ("lin1", "lin2")]
        SCAN_LINKS = 9

        def chain(eng, s, base=0):
            n = [0]

            def link_(ins):
                n[0] += 1
                ins.then_inc(s, 1)
                eng.wait_ge(s, base + n[0])
            link_.n = n
            return link_

        def rev(t):
            return t[:, ::-1]

        def bins_of(etype, step):
            _, v = nc.values_load_multi_w_load_instructions(
                bin_i[0:1, step:step + UN], engines=[etype], min_val=0, max_val=BINS - 1,
                skip_runtime_bounds_check_because="a step's bin is step - chunk, within 0..24 by the staircase")
            return v

        def slots():
            for t in range(STEPS + LAG):
                j, piece = t // BLK - 1, t % BLK
                yield (t if t < STEPS else None, (j, piece) if 0 <= j < NBLK and piece < S_SLOTS else None,
                       t - LAG if t >= LAG else None)

        @block.sync
        def _(sp):
            sp.wait_ge(S["pads_set"], 4)
            three = (CT - 1) * P
            for d, t in ((dst_d, dst_i), (src_d, src_i)):
                sp.dma_start(t[:, 0:CT - 1, :],
                             d[0:three * P].rearrange("(t p e) -> p t e", p=P, e=P)).then_inc(S["edges_in"], 16)
                sp.dma_start(t[0:FULL - three, CT - 1, :],
                             d[three * P:FULL * P].rearrange("(p e) -> p e", e=P)).then_inc(S["edges_in"], 16)
                sp.dma_start(t[FULL - three:FULL - three + 1, CT - 1, 0:TAIL],
                             d[FULL * P:EDGES].rearrange("(p e) -> p e", p=1)).then_inc(S["edges_in"], 16)
            with nc.allow_non_contiguous_dma(reason="one value of each chunk"):
                lastcol = dst_d[0:FULL * P].rearrange("(c e) -> c e", e=P)[:, P - 1:P]
                sp.dma_start(prev_i[1:P, 0:1], lastcol[0:P - 1, :]).then_inc(S["edges_in"], 16)
                for t in range(1, CT):
                    n = min(P, CHUNKS - t * P)
                    sp.dma_start(prev_i[0:n, t:t + 1],
                                 lastcol[t * P - 1:t * P - 1 + n, :]).then_inc(S["edges_in"], 16)
            sp.dma_start(x_rows[:, 0:BINS - 1, :],
                         x_d[0:(BINS - 1) * P, :].rearrange("(t p) f -> p t f", p=P)).then_inc(S["x_in"], 16)
            sp.dma_start(x_rows[0:NODES - (BINS - 1) * P, BINS - 1, :],
                         x_d[(BINS - 1) * P:NODES, :]).then_inc(S["x_in"], 16)
            sp.wait_ge(S["rows_ready"], 1)
            with nc.allow_non_contiguous_dma(reason="rows of 256 bytes"):
                sp.dma_start(dl_d.rearrange("(j r) e -> r j e", r=BLK), dl_rb[:, :, :]).then_inc(S["rows_out"], 16)
                sp.wait_ge(S["rows_out"], 16)
                sp.dma_start(first_b[:, :],
                             dl_d.rearrange("(j r) e -> j (r e)", r=BLK)[:, 0:1].rearrange("j o -> o j")
                             .to_broadcast([P, NBLK])).then_inc(S["first_in"], 16)
            dl_flat = dl_d.rearrange("(o s) e -> o (s e)", o=1)
            per_layer = STEPS // BC
            for l in range(2):
                for q in range(per_layer):
                    n = l * per_layer + q
                    if n >= 2:
                        sp.wait_ge(S["hot_t_ready"], (n - 1) * (BC // UN))
                    sp.dma_start(dl_bc[:, n % 2, :],
                                 dl_flat[:, q * BC * P:(q + 1) * BC * P].to_broadcast([P, BC * P])
                                 ).then_inc(dl_in[n % 2], 16)
                if l == 0:
                    for g in range(NGR):
                        t0, k, _ = group(g)
                        sp.wait_ge(S["back_read"], g + 1)
                        sp.dma_start(h_d.rearrange("(t p) f -> p t f", p=P)[:, t0:t0 + k, :],
                                     h_out[g % 2][:, 0:k, :]).then_inc(h_saved[g % 2], 16)
            for g in range(NGR):
                t0, k, _ = group(g)
                sp.wait_ge(S["y_ready"], g + 1)
                if t0 + k < BINS:
                    sp.dma_start(out[t0 * P:(t0 + k) * P, :].rearrange("(t p) f -> p t f", p=P),
                                 x_rows[:, t0:t0 + k, :]).then_inc(S["y_out"], 16)
                else:
                    assert k == 1
                    sp.dma_start(out[t0 * P:NODES, :], x_rows[0:NODES - t0 * P, t0, :]).then_inc(S["y_out"], 16)
            sp.wait_ge(S["y_out"], 16 * NGR)

        @block.gpsimd
        def _(pool):
            nc.gpsimd.memset(dst_i[:, CT - 1, :], PAD_NODE).then_inc(S["pads_set"], 1)
            nc.gpsimd.memset(src_i[:, CT - 1, :], 0).then_inc(S["pads_set"], 1)
            nc.gpsimd.memset(prev_i[:, 0:1], 0)
            nc.gpsimd.memset(prev_i[:, 1:CT], PAD_NODE).then_inc(S["pads_set"], 1)
            nc.gpsimd.memset(x_rows[:, BINS - 1, :], 0.0).then_inc(S["pads_set"], 1)

            def iota(t, step, n, base_step):
                return nc.gpsimd.iota(t, [[step, n]], base=0, channel_multiplier=base_step,
                                      allow_small_or_imprecise_dtypes=True)
            iota(chunk_f[:, :], P, CT, 1)
            iota(chunk128[:, :], P * P, CT, P)
            iota(step_f, 1, STEPS, 0)
            iota(step128, P, STEPS, 0)
            iota(rowstep_f[:, :], BLK, NBLK, 1)
            iota(col_f[:, :], 1, P, 0)
            iota(part_f[:, :], 0, 1, 1).then_inc(S["consts_set"], 1)
            nc.gpsimd.memset(gathered[:, 0:BLK, F:C1], 1.0).then_inc(S["ones_set"], 1)
            pool.wait_ge(S["prep_copied"], 1)
            for l, rows in enumerate((x_d, h_d)):
                if l == 1:
                    for k in range(2):
                        pool.wait_ge(h_saved[k], 16 * len(range(k, NGR, 2)))
                    nc.gpsimd.memset(gathered[:, :, F:C1], 1.0).then_inc(S["ones_set"], 1)
                for t in range(STEPS):
                    n = l * STEPS + t
                    if n == BLK:
                        pool.wait_ge(S["masks_ready"], 1)
                        pool.wait_ge(S["qk_ready"], 4)
                        nc.gpsimd.memset(gathered[:, BLK:RING, F:C1], 1.0).then_inc(S["ones_set"], 1)
                    if n >= RING:
                        pool.wait_ge(S["u_ready"], n - RING + 1)
                    if n >= GQ:
                        pool.wait_ge(got[n % GQ], 16 * (n // GQ))
                    nc.gpsimd.indirect_dma_start(
                        out=gathered[:, t % RING, 0:F], out_offset=None, in_=rows[:, :],
                        in_offset=bass.IndirectOffsetOnAxis(ap=src_e[:, t:t + 1], axis=0),
                    ).then_inc(got[n % GQ], 16)

        @block.scalar
        def _(act):
            for l in range(2):
                for n, t in enumerate((wq, wk, wv, wskip, wlin)):
                    act.dma_start(t[:, l, :], A[f"L0_gnn_{NAMES[n][l]}_w"][:, :]).then_inc(S["weights_in"], 16)
            with nc.allow_non_contiguous_dma(reason="biases as columns"):
                for l in range(2):
                    for n, t in enumerate((bq, bk)):
                        act.dma_start(t[:, l, :], A[f"L0_gnn_{NAMES[n][l]}_b"].rearrange("(h k) -> k h", h=HEADS)
                                      ).then_inc(S["weights_in"], 16)
                    act.dma_start(bv[:, l, :], A[f"L0_gnn_{NAMES[2][l]}_b"].rearrange("(h k) -> h k", h=HEADS)
                                  ).then_inc(S["weights_in"], 16)
                    for n, t in ((3, bs), (4, bl)):
                        act.dma_start(t[:, l:l + 1], A[f"L0_gnn_{NAMES[n][l]}_b"].rearrange("(k o) -> k o", o=1)
                                      ).then_inc(S["weights_in"], 16)

            for m in range(4):
                act.wait_ge(S["weights_tp"], m + 1)
                nc.scalar.copy(wqT[:, m, :], bank_t[m % 2][:, 0:F])
                nc.scalar.copy(wkT[:, m, 0:F], bank_t[m % 2][:, F:2 * F]).then_inc(S["weights_tp_copied"], 1)
            for m in range(4):
                l, h = divmod(m, 2)
                act.wait_ge(S["qk_mm"], m + 1)
                nc.scalar.mul(qk[:, l, h * C1:(h + 1) * C1], bank_u[m % 2][:, 0:C1], F ** -0.5)
                nc.scalar.mul(qk_bias[:, l, h * C1:(h + 1) * C1], bank_u[m % 2][:, 256:256 + C1],
                              F ** -0.5).then_inc(S["qk_ready"], 1)
            for g in range(NGR):
                t0, k, w = group(g)
                act.wait_ge(S["x_tp"], g + 1)
                nc.scalar.copy(xT[:, t0 * P:t0 * P + w], bank_x[g % 2][:, 0:w]).then_inc(S["xT_ready"], 1)

            def split(l):
                for g in range(NGR):
                    t0, k, _ = group(g)
                    n = l * NGR + g
                    act.wait_ge(S["t_biased"], n + 1)
                    nc.scalar.copy(table[:, t0:t0 + k, 0, :], rest[:, 0:k, :]).then_inc(S["part1"], 1)
                    act.wait_ge(S["left_ready"], n + 1)
                    nc.scalar.copy(table[:, t0:t0 + k, 1, :], left[:, 0:k, :]).then_inc(S["part2"], 1)

            def scan(l, j, piece):
                s = l * NBLK + j
                if piece == 0:
                    act.wait_ge(S["row_tp"], s + 1)
                    nc.scalar.copy(a_row[:, :, :].rearrange("p h e -> p (h e)"),
                                   bank_s[0:BLK, 0:2 * P]).then_inc(S["row_ready"], 1)
                if piece == 4:
                    act.wait_ge(S["drop_ready"], s + 1)
                    nc.scalar.activation(shrink[:, :], drop[:, 1:2], ACT.Exp,
                                         scale=-1.0).then_inc(S["shrink_ready"], 1)
                if piece == 7:
                    act.wait_ge(S["off_ready"], s + 1)
                    nc.scalar.activation(w_row[:, :, :], a_off[:, :, :], ACT.Exp).then_inc(S["w_row_ready"], 1)
                if piece == 8:
                    act.wait_ge(S["w_row_tp"], s + 1)
                    nc.scalar.copy(weight[:, j % 2, :, :].rearrange("p h e -> p (h e)"),
                                   bank_s[:, 256:256 + 2 * BLK]).then_inc(S["weight_ready"], 1)

            def weigh(l, c):
                if c % BLK == 0:
                    act.wait_ge(S["weight_ready"], l * NBLK + c // BLK + 1)
                act.wait_ge(S["hot_e_ready"], l * STEPS + c + 1)
                for h in range(HEADS):
                    last = nc.scalar.activation(whot[:, c % UN, h, :], hot_e[:, c % UN, :], ACT.Copy,
                                                scale=weight[:, c // BLK % 2, h, c % BLK:c % BLK + 1])
                last.then_inc(S["whot_ready"], 1)

            split(0)
            for l in range(2):
                for a, s, c in slots():
                    if s is not None:
                        scan(l, *s)
                    if c is not None:
                        weigh(l, c)
                for g in range(NGR + 1):
                    if g < NGR:
                        t0, k, w = group(g)
                        m = l * NGR + g
                        act.wait_ge(S["uT_tp"], m + 1)
                        nc.scalar.copy(uT[g % 2][:, 0, 0:w], bank_x[g % 2][:, 0:w])
                        nc.scalar.copy(ratio[g % 2][:, 0:w], bank_w[0:2, 0:w]).then_inc(S["uT_act"], 1)
                    if g >= 1:
                        t0, k, w = group(g - 1)
                        act.wait_ge(S["projected"], l * NGR + g)
                        nc.scalar.activation(xT[:, t0 * P:t0 * P + w], bank_p[(g - 1) % 2][:, 0:w], ACT.Identity,
                                             bias=bskip[:, l:l + 1]).then_inc(S["xT_ready"], 1)
                if l == 0:
                    split(1)
            for g in range(NGR):
                t0, k, _ = group(g)
                act.wait_ge(S["var_ready"], g + 1)
                nc.scalar.activation(std[:, t0:t0 + k], vare[:, t0:t0 + k], ACT.Sqrt).then_inc(S["std_ready"], 1)

        @block.tensor
        def _(pe):
            PE = mybir.EngineType.PE
            pe.wait_ge(S["sel_ready"], 1)
            banks = [bank_s, bank_r]
            what = [(src_f, None), (dst_f, None), (chunk_f, 1), (ends, 0), (ends, 2)]

            def prepare(r):
                if r >= 2:
                    pe.wait_ge(S["prep_copied"], r - 1)
                b = banks[r % 2]
                if r < 5:
                    src, c = what[r]
                    for t in range(CT):
                        lhsT = src[:, t:t + 1] if r == 2 else src[:, t, :] if c is None else src[:, t, c:c + 2]
                        rows = 1 if r == 2 else P if c is None else 2
                        last = nc.tensor.matmul(b[0:rows, 0:STEPS], lhsT, sel[:, t, :],
                                                start=(t == 0), stop=(t == CT - 1))
                else:
                    for j in range(4 * (r - 5), 4 * (r - 5) + 4):
                        for t in range(CT):
                            last = nc.tensor.matmul(b[0:BLK, (j % 4) * P:(j % 4 + 1) * P],
                                                    sel[:, t, j * BLK:(j + 1) * BLK], dst_f[:, t, :],
                                                    start=(t == 0), stop=(t == CT - 1))
                last.then_inc(S["prep_mm"], 1)
            prepare(0)
            prepare(1)
            pe.wait_ge(S["ident_ready"], 1)
            pe.wait_ge(S["weights_in"], 16 * N_WEIGHT_DMA)
            for m in range(4):
                l, h = divmod(m, 2)
                if m >= 2:
                    pe.wait_ge(S["weights_tp_copied"], m - 1)
                nc.tensor.transpose(bank_t[m % 2][:, 0:F], wq[:, l, h * F:(h + 1) * F], ident[:, :])
                nc.tensor.transpose(bank_t[m % 2][:, F:2 * F], wk[:, l, h * F:(h + 1) * F],
                                    ident[:, :]).then_inc(S["weights_tp"], 1)
            for r in range(2, PREP):
                prepare(r)
            pe.wait_ge(S["wk_bias"], 1)
            for m in range(4):
                l, h = divmod(m, 2)
                pe.wait_ge(S["weights_tp_copied"], m + 1)
                if m >= 2:
                    pe.wait_ge(S["qk_ready"], m - 1)
                nc.tensor.matmul(bank_u[m % 2][:, 0:C1], wqT[:, m, :], wkT[:, m, :], start=True, stop=True)
                pe.wait_ge(S["bq_ready"], m + 1)
                nc.tensor.matmul(bank_u[m % 2][:, 256:256 + C1], bq_wide, wkT[:, m, :],
                                 start=True, stop=True).then_inc(S["qk_mm"], 1)
            pe.wait_ge(S["x_in"], 32)
            for g in range(NGR):
                t0, k, w = group(g)
                if g >= 2:
                    pe.wait_ge(S["xT_ready"], g - 1)
                for t in range(k):
                    last = nc.tensor.transpose(bank_x[g % 2][:, t * P:(t + 1) * P], x_rows[:, t0 + t, :], ident[:, :])
                last.then_inc(S["x_tp"], 1)

            def make_t(l):
                for g in range(NGR):
                    t0, k, _ = group(g)
                    n = l * NGR + g
                    if l == 0:
                        pe.wait_ge(S["xT_ready"], n + 1)
                    if g >= 1:
                        pe.wait_ge(S["t_biased"], n)
                    for t in range(k):
                        last = nc.tensor.matmul(bank_T[:, t, 0:CW], xT[:, (t0 + t) * P:(t0 + t + 1) * P],
                                                qk[:, l, :], start=True, stop=True)
                    last.then_inc(S["t_mm"], 1)
            pe.wait_ge(S["qk_ready"], 4)
            pe.wait_ge(S["prep_copied"], PREP)
            make_t(0)

            def step_t(l, t, b):
                n = l * STEPS + t
                if t % UN == 0:
                    pe.wait_ge(S["hot_t_ready"], n // UN + 1)
                if n >= NB:
                    pe.wait_ge(S["alpha_ready"], n - NB + 1)
                for part in range(3):
                    last = nc.tensor.matmul(bank_t[n % NB][:, 0:CW], hot_t[:, n // UN % 2, t % UN, :],
                                            table[:, bass.ds(b, 1), part, :].rearrange("p o c -> p (o c)"),
                                            start=(part == 0), stop=(part == 2))
                last.then_inc(S["t_ready"], 1)

            def step_u(l, c):
                n = l * STEPS + c
                if n >= NB:
                    pe.wait_ge(S["u_added"], n - NB + 1)
                pe.wait_ge(S["whot_ready"], n + 1)
                for h in range(HEADS):
                    last = nc.tensor.matmul(bank_u[n % NB][:, h * C1:(h + 1) * C1], whot[:, c % UN, h, :],
                                            gathered[:, c % RING, :], start=True, stop=True)
                last.then_inc(S["u_ready"], 1)

            def scan(l, j, piece):
                s = l * NBLK + j
                if piece == 0:
                    pe.wait_ge(S["alpha_ready"], l * STEPS + (j + 1) * BLK)
                    for h in range(HEADS):
                        last = nc.tensor.transpose(bank_s[0:BLK, h * P:(h + 1) * P], alpha[:, j % 2, h, :], ident[:, :])
                    last.then_inc(S["row_tp"], 1)
                if piece == 2:
                    pe.wait_ge(S["m_end_ready"], s + 1)
                    for n in range(2):
                        last = nc.tensor.transpose(bank_r[0:2, n * 64:n * 64 + BLK], m_end[:, 2 * n:2 * n + 2],
                                                   ident[0:BLK, 0:BLK])
                    last.then_inc(S["m_end_tp"], 1)
                if piece == 4:
                    pe.wait_ge(S["link_m_ready"], s + 1)
                    for n in range(2):
                        last = nc.tensor.transpose(bank_r[0:BLK, 256 + 2 * n:258 + 2 * n], link_m[:, n, :],
                                                   ident[0:2, 0:2])
                    last.then_inc(S["link_tp"], 1)
                if piece == 6:
                    pe.wait_ge(S["shrink_d_ready"], s + 1)
                    nc.tensor.matmul(bank_r[:, 300:302], ones[:, :], shrink_d[:, :],
                                     start=True, stop=True).then_inc(S["factor_mm"], 1)
                if piece == 8:
                    pe.wait_ge(S["w_row_ready"], s + 1)
                    for h in range(HEADS):
                        last = nc.tensor.transpose(bank_s[:, 256 + h * BLK:256 + (h + 1) * BLK], w_row[:, h, :],
                                                   ident[0:BLK, 0:BLK])
                    last.then_inc(S["w_row_tp"], 1)

            for l in range(2):
                for a, s, c in slots():
                    if a is not None:
                        if a % UN == 0:
                            b = bins_of(PE, a)
                        if a < BINS and a % G == 0:
                            pe.wait_ge(S["part3"], l * NGR + a // G + 1)
                        step_t(l, a, b[a % UN])
                    if s is not None:
                        scan(l, *s)
                    if c is not None:
                        step_u(l, c)
                for g in range(NGR + 2):
                    if g < NGR:
                        t0, k, w = group(g)
                        m = l * NGR + g
                        pe.wait_ge(S["un_ready"], m + 1)
                        if g >= 1:
                            pe.wait_ge(S["uT_act"], m)
                            pe.wait_ge(S["uT_dve"], m)
                        for t in range(k):
                            for h in range(HEADS):
                                nc.tensor.transpose((bank_x[g % 2], bank_h1)[h][:, t * P:(t + 1) * P],
                                                    u_n[g % 2][:, t * HEADS + h, 0:F], ident[:, :])
                            last = nc.tensor.transpose(bank_w[0:2, t * P:(t + 1) * P],
                                                       u_n[g % 2][:, t * HEADS:(t + 1) * HEADS, F], ident[:, :])
                        last.then_inc(S["uT_tp"], 1)
                    if 1 <= g <= NGR:
                        q = g - 1
                        t0, k, w = group(q)
                        m = l * NGR + q
                        pe.wait_ge(S["uT_act"], m + 1)
                        pe.wait_ge(S["uT_dve"], m + 1)
                        if q >= 2:
                            pe.wait_ge(S["xT_ready"], NGR + m - 1)
                        o = bank_p[q % 2][:, 0:w]
                        nc.tensor.matmul(o, wskip[:, l, :], xT[:, t0 * P:t0 * P + w], start=True, stop=False)
                        for h in range(HEADS):
                            nc.tensor.matmul(o, wv[:, l, h * F:(h + 1) * F], uT[q % 2][:, h, 0:w],
                                             start=False, stop=False)
                        nc.tensor.matmul(o, bv[:, l, :], ratio[q % 2][:, 0:w],
                                         start=False, stop=True).then_inc(S["projected"], 1)
                    if g >= 2:
                        q = g - 2
                        t0, k, w = group(q)
                        m = l * NGR + q
                        pe.wait_ge(S["xT_ready"], NGR + m + 1)
                        if m >= 1:
                            pe.wait_ge(S["back_read"], m)
                        for t in range(k):
                            last = nc.tensor.transpose(bank_b[:, t * P:(t + 1) * P],
                                                       xT[:, (t0 + t) * P:(t0 + t + 1) * P], ident[:, :])
                        last.then_inc(S["back_tp"], 1)
                if l == 0:
                    pe.wait_ge(S["back_read"], NGR)
                    make_t(1)

        @block.vector
        def _(dve):
            DVE = mybir.EngineType.DVE
            V = nc.vector
            step = chain(dve, S["dve_step"])
            dve.wait_ge(S["consts_set"], 1)
            V.tensor_scalar(rowstep128[:, :], rowstep_f[:, :], float(P), None, ALU.mult)
            V.tensor_scalar(ident[:, :], col_f[:, :], part_f[:, 0:1], None, ALU.is_equal).then_inc(S["ident_ready"], 1)

            dve.wait_ge(S["edges_in"], 16 * N_EDGE_DMA)
            V.tensor_scalar(lastbin_i[:, :], dst_i[:, :, P - 1], 7, None, ALU.arith_shift_right)
            V.tensor_scalar(prevbin_i[:, :], prev_i[:, :], 7, None, ALU.arith_shift_right)
            step(V.tensor_copy(src_f[:, :, :], src_i[:, :, :]))
            V.tensor_tensor(key[:, :], lastbin_i[:, :], chunk_f[:, :], ALU.add)
            V.scalar_tensor_tensor(out=keyprev[:, :], in0=prevbin_i[:, :], scalar=-1.0, in1=chunk_f[:, :],
                                   op0=ALU.add, op1=ALU.add)
            for t in range(CT):
                last = V.tensor_scalar(dst_f[:, t, :], dst_i[:, t, :], chunk128[:, t:t + 1], None, ALU.add)
            step(last)
            for t in range(CT):
                last = V.tensor_scalar(before[:, t, :], step_f, key[:, t:t + 1], None, ALU.is_le)
            step(last)
            V.tensor_copy(ends[:, :, 0:2], dst_f[:, :, 0:1].to_broadcast([P, CT, 2]))
            V.tensor_copy(ends[:, :, 2:4], dst_f[:, :, P - 1:P].to_broadcast([P, CT, 2]))
            for t in range(CT):
                last = V.scalar_tensor_tensor(out=sel[:, t, :], in0=step_f, scalar=keyprev[:, t:t + 1],
                                              in1=before[:, t, :], op0=ALU.is_gt, op1=ALU.mult)
            last.then_inc(S["sel_ready"], 1)
            V.tensor_copy(col_b[:, :], col_f[:, :])
            V.memset(ones[:, :], 1.0)
            V.memset(run_b[:, :], -BIG)
            V.memset(link[:, :], 0.0)
            V.memset(seg_f[:, :, 0:1], 0.0)
            V.memset(seg_b[:, :, 0:1], 0.0)

            def copied(r, ins):
                ins.then_inc(S["prep_copied"], 1)
            dve.wait_ge(S["prep_mm"], 1)
            copied(0, V.tensor_copy(src_e[:, :], bank_s[:, 0:STEPS]))
            dve.wait_ge(S["prep_mm"], 2)
            copied(1, V.tensor_tensor(dl_e[:, :], bank_r[:, 0:STEPS], step128, ALU.subtract))

            dve.wait_ge(S["weights_in"], 16 * N_WEIGHT_DMA)
            V.tensor_tensor(wskip[:, :, :], wskip[:, :, :], wlin[:, :, :], ALU.add)
            V.tensor_tensor(bskip[:, :], bs[:, :], bl[:, :], ALU.add)
            V.tensor_copy(wkT[:, :, F], bk[:, :, :].rearrange("p l h -> p (l h)")).then_inc(S["wk_bias"], 1)
            V.tensor_copy(bq_wide, bq[:, 0, 0:1].to_broadcast([P, P])).then_inc(S["bq_ready"], 1)
            dve.wait_ge(S["prep_mm"], 3)
            copied(2, V.tensor_tensor(bin_i[:, :], step_f[0:1], bank_s[0:1, 0:STEPS], ALU.subtract))
            dve.wait_ge(S["prep_mm"], 4)
            copied(3, V.tensor_tensor(firsts, bank_r[0:2, 0:STEPS], step128[0:2], ALU.subtract))
            dve.wait_ge(S["prep_mm"], 5)
            copied(4, V.tensor_tensor(lasts, bank_s[0:2, 0:STEPS], step128[0:2], ALU.subtract))
            for r in range(2):
                dve.wait_ge(S["prep_mm"], 6 + r)
                for j in range(4 * r, 4 * r + 4):
                    last = V.tensor_scalar(dl_r[:, j, :], (bank_r, bank_s)[r][0:BLK, (j % 4) * P:(j % 4 + 1) * P],
                                           rowstep128[0:BLK, j:j + 1], None, ALU.subtract)
                copied(5 + r, last)
            dve.wait_ge(S["prep_copied"], PREP)
            V.tensor_copy(dl_rb, dl_r).then_inc(S["rows_ready"], 1)
            for m in range(1, 4):
                dve.wait_ge(S["qk_mm"], m)
                V.tensor_copy(bq_wide, bq[:, m // 2, m % 2:m % 2 + 1].to_broadcast([P, P])
                              ).then_inc(S["bq_ready"], 1)

            def penalty(o, i):
                return V.tensor_scalar(o, i, 1.0, BIG, ALU.subtract, ALU.mult)
            V.tensor_tensor(same[:, :, 0:P - 1], dl_r[:, :, 1:P], dl_r[:, :, 0:P - 1], ALU.is_equal)
            V.tensor_tensor(in_last[:, :, :], dl_r, dl_r[:, :, P - 1:P].to_broadcast([BLK, NBLK, P]), ALU.is_equal)
            V.tensor_tensor(in_first[:, :, :], dl_r, dl_r[:, :, 0:1].to_broadcast([BLK, NBLK, P]), ALU.is_equal)
            V.tensor_tensor(link[:, 1:STEPS], lasts[:, 0:STEPS - 1], firsts[:, 1:STEPS], ALU.is_equal)
            step(V.tensor_tensor(single, firsts, lasts, ALU.is_equal))
            penalty(seg_f[:, :, 1:P], same[:, :, 0:P - 1])
            penalty(seg_b[:, :, 1:P], same[:, :, P - 2::-1])
            penalty(linkneg[:, :], link[:, :])
            V.tensor_tensor(carry_f[:, :], link[:, 0:STEPS], single, ALU.mult)
            step(V.tensor_tensor(joined, link[:, 1:STEPS + 1], single, ALU.mult))
            penalty(in_last[:, :, :], in_last[:, :, :])
            penalty(in_first[:, :, :], in_first[:, :, :])
            penalty(carry_f[:, :], carry_f[:, :])
            step(penalty(carry_b[:, :, :], joined.rearrange("p (j r) -> p j r", r=BLK)[:, :, ::-1]))

            def split(l):
                for g in range(NGR):
                    t0, k, _ = group(g)
                    n = l * NGR + g
                    dve.wait_ge(S["t_mm"], n + 1)
                    if n >= 1:
                        dve.wait_ge(S["part3"], n)
                    V.tensor_tensor(rest[:, 0:k, :], bank_T[:, 0:k, 0:CW],
                                    qk_bias[:, l:l + 1, :].to_broadcast([P, k, CW]), ALU.add).then_inc(S["t_biased"], 1)
                    dve.wait_ge(S["part1"], n + 1)
                    V.tensor_tensor(left[:, 0:k, :], rest[:, 0:k, :], table[:, t0:t0 + k, 0, :],
                                    ALU.subtract).then_inc(S["left_ready"], 1)
                    dve.wait_ge(S["part2"], n + 1)
                    V.tensor_tensor(table[:, t0:t0 + k, 2, :], left[:, 0:k, :], table[:, t0:t0 + k, 1, :],
                                    ALU.subtract).then_inc(S["part3"], 1)
            split(0)
            dve.wait_ge(S["first_in"], 16)
            V.tensor_scalar(first_hot[:, :], first_b[:, :], part_f[:, 0:1], None,
                            ALU.is_equal).then_inc(S["masks_ready"], 1)

            def one_hot_t(q):
                n = q // (BC // UN)
                part = q % (BC // UN)
                if part == 0:
                    dve.wait_ge(dl_in[n % 2], 16 * (n // 2 + 1))
                V.tensor_scalar(hot_t[:, q % 2, :, :].rearrange("p k e -> p (k e)"),
                                dl_bc[:, n % 2, part * UN * P:(part + 1) * UN * P], part_f[:, 0:1], None,
                                ALU.is_equal).then_inc(S["hot_t_ready"], 1)

            def one_hot_e(l, c):
                V.tensor_scalar(hot_e[:, c % UN, :], col_b[:, :], dl_e[:, c:c + 1], None,
                                ALU.is_equal).then_inc(S["hot_e_ready"], 1)

            def step_alpha(l, t):
                n = l * STEPS + t
                if n >= UN:
                    dve.wait_ge(S["alpha_ready"], n - UN + 1)
                dve.wait_ge(got[n % GQ], 16 * (n // GQ + 1))
                dve.wait_ge(S["t_ready"], n + 1)
                for h in range(HEADS):
                    last = V.scalar_tensor_tensor(
                        out=junk[:, t % UN, h, :], in0=bank_t[n % NB][:, h * C1:(h + 1) * C1], scalar=1.0,
                        in1=gathered[:, t % RING, :], op0=ALU.mult, op1=ALU.mult,
                        accum_out=alpha[:, t // BLK % 2, h, t % BLK:t % BLK + 1])
                last.then_inc(S["alpha_ready"], 1)

            def step_add(l, c, b):
                n = l * STEPS + c
                if n >= 1:
                    dve.wait_ge(S["u_added"], n)
                dve.wait_ge(S["u_ready"], n + 1)
                bin_acc = acc[:, bass.ds(b, 1), :].rearrange("p o c -> p (o c)")
                V.tensor_tensor(bin_acc, bank_u[n % NB][:, 0:CW], bin_acc, ALU.add).then_inc(S["u_added"], 1)

            def scan(l, j, piece):
                s = l * NBLK + j
                ln = chain(dve, S["scan_step"], s * SCAN_LINKS + {1: 0, 3: 1, 5: 4, 6: 6, 7: 7}.get(piece, 0))
                p0 = j * BLK
                if piece == 1:
                    dve.wait_ge(S["row_ready"], s + 1)
                    for n, mask in enumerate((in_last, in_first)):
                        last = V.tensor_tensor(a_end[:, 2 * n:2 * n + 2, :], a_row[:, :, :],
                                               mask[:, j:j + 1, :].to_broadcast([BLK, HEADS, P]), ALU.add)
                    ln(last)
                    V.tensor_reduce(m_end[:, :], a_end[:, :, :], AX, ALU.max).then_inc(S["m_end_ready"], 1)
                if piece == 3:
                    dve.wait_ge(S["m_end_tp"], s + 1)
                    V.tensor_tensor_scan(run_f[:, 1:BLK + 1], carry_f[:, p0:p0 + BLK], bank_r[0:2, 0:BLK],
                                         run_f[:, 0:1], ALU.add, ALU.max)
                    ln(V.tensor_tensor_scan(rev(run_b[:, 0:BLK]), carry_b[:, j, :], rev(bank_r[0:2, 64:64 + BLK]),
                                            -BIG, ALU.add, ALU.max))
                    V.tensor_tensor(link_m[:, 0, :], run_f[:, 0:BLK], linkneg[:, p0:p0 + BLK], ALU.add)
                    V.tensor_tensor(link_m[:, 1, :], run_b[:, 1:BLK + 1], linkneg[:, p0 + 1:p0 + BLK + 1],
                                    ALU.add).then_inc(S["link_m_ready"], 1)
                    ln(V.scalar_tensor_tensor(out=drop[:, 0:1], in0=run_b[:, 0:1], scalar=run_f[:, 0:1],
                                              in1=run_f[:, 0:1], op0=ALU.max, op1=ALU.subtract))
                    V.tensor_tensor(drop[:, 1:2], drop[:, 0:1], link[:, p0:p0 + 1], ALU.mult).then_inc(S["drop_ready"], 1)
                    ln(V.tensor_copy(run_f[:, 0:1], run_f[:, BLK:BLK + 1]))
                if piece == 5:
                    dve.wait_ge(S["link_tp"], s + 1)
                    ln(V.tensor_copy(link_c[:, :], bank_r[0:BLK, 256:260]))
                    dve.wait_ge(S["shrink_ready"], s + 1)
                    V.tensor_scalar(shrink_d[:, :], ident[0:2, 0:2], shrink[:, 0:1], None,
                                    ALU.mult).then_inc(S["shrink_d_ready"], 1)
                    for h in range(HEADS):
                        V.tensor_tensor_scan(max_f[:, h, :], seg_f[:, j, :], a_row[:, h, :],
                                             link_c[:, h:h + 1], ALU.add, ALU.max)
                        last = V.tensor_tensor_scan(rev(max_b[:, h, :]), seg_b[:, j, :], rev(a_row[:, h, :]),
                                                    link_c[:, 2 + h:3 + h], ALU.add, ALU.max)
                    last.then_inc(S["scan_step"], 1)
                if piece == 6:
                    dve.wait_ge(S["scan_step"], s * SCAN_LINKS + 6)
                    ln(V.tensor_tensor(max_s[:, :, :], max_f[:, :, :], max_b[:, :, :], ALU.max))
                    V.tensor_tensor(a_off[:, :, :], a_row[:, :, :], max_s[:, :, :], ALU.subtract
                                    ).then_inc(S["off_ready"], 1)
                if piece == 7:
                    dve.wait_ge(S["factor_mm"], s + 1)
                    ln(V.tensor_scalar(shrink_1[:, :], bank_r[:, 300:302], 1.0, None, ALU.subtract))
                    V.tensor_scalar(factor[:, :], shrink_1[:, :], first_hot[:, j:j + 1], 1.0,
                                    ALU.mult, ALU.add).then_inc(S["scan_step"], 1)

            def rescale(l, j, b):
                s = l * NBLK + j
                dve.wait_ge(S["scan_step"], (s + 1) * SCAN_LINKS)
                if s > 0:
                    dve.wait_ge(S["u_added"], l * STEPS + j * BLK)
                for h in range(HEADS):
                    o = acc[:, bass.ds(b, 1), h * C1:(h + 1) * C1].rearrange("p o c -> p (o c)")
                    last = V.tensor_scalar(o, o, factor[:, h:h + 1], None, ALU.mult)
                last.then_inc(S["ends_ready"], 1)
                dve.wait_ge(S["ends_ready"], s + 1)

            dve.wait_ge(S["prep_copied"], PREP)
            step(V.memset(run_f[:, 0:1], -BIG))
            AHEAD = 2
            for l in range(2):
                if l == 1:
                    split(1)
                    step(V.memset(run_f[:, 0:1], -BIG))
                V.memset(acc[:, :, :], 0.0).then_inc(S["acc_clear"], 1)
                dve.wait_ge(S["ones_set"], 1 if l == 0 else 3)
                q0 = l * (STEPS // UN)
                one_hot_t(q0)
                for a, s, c in slots():
                    if l == 0 and a == BLK:
                        dve.wait_ge(S["ones_set"], 2)
                    if a is not None:
                        if a % UN == 1 and a // UN + 1 < STEPS // UN:
                            one_hot_t(q0 + a // UN + 1)
                        step_alpha(l, a)
                    if s is not None:
                        scan(l, *s)
                    if c is None:
                        continue
                    if c == 0:
                        for k in range(AHEAD):
                            one_hot_e(l, k)
                        dve.wait_ge(S["acc_clear"], l + 1)
                    if c + AHEAD < STEPS:
                        one_hot_e(l, c + AHEAD)
                    if c >= 1:
                        step_add(l, c - 1, b[(c - 1) % UN])
                    if c % UN == 0:
                        b = bins_of(DVE, c)
                    if c % BLK == 0:
                        rescale(l, c // BLK, b[0])
                step_add(l, STEPS - 1, b[UN - 1])
                dve.wait_ge(S["u_added"], (l + 1) * STEPS)

                def normalise(g):
                    t0, k, _ = group(g)
                    m = l * NGR + g
                    sums = acc[:, t0:t0 + k, :].rearrange("p t (h c) -> p (t h) c", h=HEADS)
                    d, r = den[:, g, 0:2 * k], rden[:, g, 0:2 * k]
                    if g >= 2:
                        dve.wait_ge(S["uT_tp"], m - 1)
                    ln = chain(dve, S["node_step"], 2 * m)
                    ln(V.tensor_scalar(d, sums[:, :, F], 1e-16, float(HEADS), ALU.add, ALU.mult))
                    ln(V.reciprocal(r, d))
                    V.tensor_tensor(u_n[g % 2][:, 0:2 * k, :], sums,
                                    r.rearrange("p (t o) -> p t o", o=1).to_broadcast([P, 2 * k, C1]),
                                    ALU.mult).then_inc(S["un_ready"], 1)
                normalise(0)
                for g in range(NGR + 2):
                    if g + 1 < NGR:
                        normalise(g + 1)
                    if g < NGR:
                        t0, k, w = group(g)
                        dve.wait_ge(S["uT_tp"], l * NGR + g + 1)
                        if g >= 2:
                            dve.wait_ge(S["projected"], l * NGR + g - 1)
                        V.tensor_copy(uT[g % 2][:, 1, 0:w], bank_h1[:, 0:w]).then_inc(S["uT_dve"], 1)
                    if g >= 2:
                        q = g - 2
                        t0, k, w = group(q)
                        dve.wait_ge(S["back_tp"], l * NGR + q + 1)
                        if l == 0:
                            if q >= 2:
                                dve.wait_ge(h_saved[q % 2], 16 * (q // 2))
                            V.tensor_copy(h_out[q % 2][:, 0:k, :].rearrange("p t f -> p (t f)"),
                                          bank_b[:, 0:w]).then_inc(S["back_read"], 1)
                        else:
                            rows = x_rows[:, t0:t0 + k, :]
                            V.tensor_tensor(rows, rows, bank_b[:, 0:w].rearrange("p (t f) -> p t f", t=k),
                                            ALU.add).then_inc(S["back_read"], 1)
                            dve.wait_ge(S["back_read"], l * NGR + q + 1)
                            for t in range(t0, t0 + k):
                                last = V.bn_stats(stats[:, t, :], x_rows[:, t, :])
                            step(last)
                            for t in range(t0, t0 + k):
                                last = V.bn_aggr(mv[:, t, :], stats[:, t, :])
                            step(last)
                            V.tensor_scalar(vare[:, t0:t0 + k], mv[:, t0:t0 + k, 1], EPS_LN, None,
                                            ALU.add).then_inc(S["var_ready"], 1)
            for g in range(NGR):
                t0, k, w = group(g)
                dve.wait_ge(S["std_ready"], g + 1)
                step(V.reciprocal(rstd[:, t0:t0 + k], std[:, t0:t0 + k]))
                for t in range(t0, t0 + k):
                    last = V.tensor_scalar(x_rows[:, t, :], x_rows[:, t, :], mv[:, t, 0:1], rstd[:, t:t + 1],
                                           ALU.subtract, ALU.mult)
                last.then_inc(S["y_ready"], 1)


_INS = ["x", "src", "dst"] + [f"L0_gnn_{n}_{k}" for n in ("q1", "k1", "v1", "s1", "q2", "k2", "v2", "s2", "lin1", "lin2")
                              for k in ("w", "b")]


def kernel(**inputs):
    import numpy as _np
    import concourse.bacc as _bacc
    from concourse import mybir as _mybir
    from concourse.bass_utils import run_bass_kernel_spmd as _run

    nc = _bacc.Bacc("TRN2", target_bir_lowering=False, num_devices=1)
    arrays, args = {}, {}
    for name in _INS:
        a = _np.ascontiguousarray(inputs[name])
        arrays[f"in_{name}"] = a
        args[name] = nc.dram_tensor(f"in_{name}", a.shape, _mybir.dt.from_np(a.dtype), kind="ExternalInput").ap()
    out = nc.dram_tensor("out", (NODES, F), _mybir.dt.float32, kind="ExternalOutput").ap()
    program(nc, args, out)
    r = _run(nc, [arrays], core_ids=[0])
    return r.results[0]["out"]
```

```python
import concourse.bass as bass
import numpy as np
from concourse import mybir
from concourse.alu_op_type import AluOpType as ALU
from contextlib import ExitStack

P = 128
NODES, EDGES, F, HEADS = 3125, 50000, 128, 2
CHUNKS = -(-EDGES // P)
BINS = -(-NODES // P)
SLOTS = BINS * P
PAD_NODE = SLOTS - 1
FULL = EDGES // P
TAIL = EDGES - FULL * P
CT = -(-CHUNKS // P)
SIZES = (26, 36, 44) + 4 * (48,) + (44, 40, 34)
STARTS = tuple(int(n) for n in np.cumsum((0,) + SIZES))
NBLK, BLK, STEPS = len(SIZES), max(SIZES), STARTS[-1]
RING = 98
UN = 4
BC = 8
GQ = 8
S_SLOTS = 9
DVE_EVERY = 6
TAIL_SLOTS = 24
NB = 3
G = 4
BR = G * HEADS + 2
ENDS = 65
MASK_TILE = 12
PE_AHEAD = 1
SKIP_SLOT, SKIP_EVERY = 5, 3
T_AHEAD = 2
LATE_ROWS, LATE_DST, LATE_MASKS = 1, 6, 7
NGR = -(-BINS // G)
C1 = F + 1
CW = HEADS * C1
ROW_SETS = -(-NBLK // G)
BIG = 1e30
EPS_LN = 1e-5
FAR = -1e4
BLOCK_OF = tuple(j for j in range(NBLK) for _ in range(SIZES[j]))
assert CHUNKS + BINS - 1 <= STEPS and STEPS % BC == 0
assert LATE_ROWS + 2 * (ROW_SETS - 1) < LATE_DST and LATE_MASKS + T_AHEAD + 2 <= MASK_TILE
assert LATE_MASKS + 2 + BINS <= SIZES[0] + S_SLOTS


def group(g):
    k = min(G, BINS - g * G)
    return g * G, k, k * P


def program(nc, A, out):
    f32, i32, bf16 = mybir.dt.float32, mybir.dt.int32, mybir.dt.bfloat16
    ACT = mybir.ActivationFunctionType
    AX = mybir.AxisListType.X
    x_d, src_d, dst_d = A["x"], A["src"], A["dst"]
    h_d = nc.dram_tensor("h_rows", (SLOTS, F), f32, kind="Internal").ap()
    dl_d = nc.dram_tensor("local_dst_rows", (STEPS, P), bf16, kind="Internal").ap()

    ctx = ExitStack()
    with ctx:
        def sb(name, shape, dt=f32):
            return ctx.enter_context(nc.sbuf_tensor(name, shape, dt))

        def sem(name):
            return ctx.enter_context(nc.semaphore(name))

        x_rows = sb("x_rows", [P, BINS, F])
        xT = sb("xT", [P, SLOTS])
        gathered = sb("gathered", [P, RING, C1])
        table = sb("table", [P, BINS, 3, CW], bf16)
        acc = sb("acc", [P, BINS, CW])

        def lender(whole):
            used = [0]

            def lend(shape, dt=f32):
                n = int(np.prod(shape))
                w = n // 2 if dt == bf16 else n
                v = whole[:, used[0]:used[0] + w]
                used[0] += w
                v = v if dt == f32 else v.bitcast(dt)
                if len(shape) == 2:
                    v = v.rearrange("p (a b) -> p a b", a=shape[0])
                if len(shape) == 3:
                    v = v.rearrange("p (a b c) -> p a b c", a=shape[0], b=shape[1])
                return v
            return lend

        tmp = lender(acc[:, :, :].rearrange("p t c -> p (t c)"))
        src_i = tmp([CT, P], i32)
        dst_i = tmp([CT, P], i32)
        src_f = tmp([CT, P])
        dst_f = tmp([CT, P])
        before = tmp([CT, STEPS])
        sel = tmp([CT, STEPS])
        step_f = tmp([STEPS])
        step128 = tmp([STEPS])
        ends = sb("ends", [P, CT, ENDS])
        table_f = table[:, :, :, :].rearrange("p t a c -> p t (a c)").bitcast(f32)
        tmp = lender(table_f[:, 0:MASK_TILE, :].rearrange("p t c -> p (t c)"))
        wq = tmp([2, HEADS * F])
        wk = tmp([2, HEADS * F])
        wqT = tmp([4, F])
        wkT = tmp([4, C1])
        wlin = tmp([2, F])
        bq_wide = tmp([P])
        qk_bias = tmp([2, CW])
        tmp = lender(table_f[:, MASK_TILE:BINS, :].rearrange("p t c -> p (t c)"))
        dl_r = tmp([NBLK, P])[0:BLK]
        dl_rb = tmp([NBLK, P], bf16)[0:BLK]
        same = tmp([NBLK, P], bf16)[0:BLK]
        firsts = tmp([STEPS])[0:2]
        lasts = tmp([STEPS])[0:2]
        single = tmp([STEPS])[0:2]
        joined = tmp([STEPS])[0:2]
        tmp = lender(table_f[:, 0:MASK_TILE, :].rearrange("p t c -> p (t c)"))
        skip = tmp([BINS, F])
        tmp = lender(table_f[:, MASK_TILE:BINS, :].rearrange("p t c -> p (t c)"))
        h_out = [tmp([G, F]) for _ in range(2)]
        tmp = lender(gathered[:, :, :].rearrange("p s c -> p (s c)"))
        u_n = [tmp([G * HEADS, C1]) for _ in range(2)]
        uT = [tmp([HEADS, G * P]) for _ in range(2)]
        den = tmp([NGR, G * HEADS])
        rden = tmp([NGR, G * HEADS])
        stats = tmp([BINS, 6])
        mv = tmp([BINS, 2])
        vare = tmp([BINS])
        std = tmp([BINS])
        rstd = tmp([BINS])
        shift = tmp([BINS])

        prev_i = sb("prev_i", [P, CT], i32)
        lastbin_i = sb("lastbin_i", [P, CT], i32)
        prevbin_i = sb("prevbin_i", [P, CT], i32)
        chunk_f = sb("chunk_f", [P, CT])
        chunk128 = sb("chunk128", [P, CT])
        key = sb("key", [P, CT])
        keyprev = sb("keyprev", [P, CT])
        part128 = sb("part128", [P, 1])
        src_e = sb("src_e", [P, STEPS], i32)
        ndl_e = sb("ndl_e", [P, STEPS])
        bin_i = sb("bin_i", [1, STEPS], i32)
        link = sb("link", [2, STEPS + 1])
        linkneg = sb("linkneg", [2, STEPS + 1])
        carry_f = sb("carry_f", [2, STEPS])
        carry_b = sb("carry_b", [2, STEPS])
        seg_f = sb("seg_f", [BLK, NBLK, P], bf16)
        seg_b = sb("seg_b", [BLK, NBLK, P], bf16)
        in_last = sb("in_last", [BLK, NBLK, P], bf16)
        in_first = sb("in_first", [BLK, NBLK, P], bf16)
        first_hot = sb("first_hot", [P, NBLK])
        ident = sb("ident", [P, P])
        ones = sb("ones", [2, P])
        zeros = sb("zeros", [P, CW])
        col_f = sb("col_f", [P, P])
        col_b = sb("col_b", [P, P], bf16)
        ncol_b = sb("ncol_b", [P, P], bf16)
        part_f = sb("part_f", [P, 1])
        wv = sb("wv", [P, 2, HEADS * F])
        wskip = sb("wskip", [P, 2, F])
        bq = sb("bq", [P, 2, HEADS])
        bk = sb("bk", [P, 2, HEADS])
        bias_rows = sb("bias_rows", [BR, 2, G * F])
        ratio = sb("ratio", [BR, 2, P])
        qk = sb("qk", [P, 2, CW])
        bias3 = sb("bias3", [65, 2, CW], bf16)
        ones_b = sb("ones_b", [65, P], bf16)
        dl_bc = sb("dl_bc", [P, 2, BC * P], bf16)
        hot_t = sb("hot_t", [P, 2, BC, P], bf16)
        apart = sb("apart", [P, UN, P], bf16)
        whot = sb("whot", [P, UN, HEADS, P])
        junk = sb("junk", [P, 2, HEADS, C1])
        alpha = sb("alpha", [P, 2, HEADS, BLK])
        below = sb("below", [P, 2, HEADS, BLK])
        a_row = sb("a_row", [BLK, HEADS, P])
        a_end = sb("a_end", [BLK, 4, P])
        m_end = sb("m_end", [BLK, 4])
        run_f = sb("run_f", [2, BLK + 1])
        run_b = sb("run_b", [2, BLK + 1])
        link_m = sb("link_m", [2, 2, BLK])
        link_c = sb("link_c", [BLK, 4])
        max_f = sb("max_f", [BLK, HEADS, P])
        max_b = sb("max_b", [BLK, HEADS, P])
        max_s = sb("max_s", [BLK, HEADS, P])
        a_off = sb("a_off", [BLK, HEADS, P])
        drop = sb("drop", [2, 2])
        shrink = sb("shrink", [2, 1])
        shrink_d = sb("shrink_d", [2, 2])
        shrink_1 = sb("shrink_1", [P, 2])
        factor = sb("factor", [P, 2])
        left = sb("left", [P, 2, CW])

        ps = ctx.enter_context(nc.psum_tensor("ps", [P, 8, 512], f32))
        bank_t = [ps[:, i, :] for i in (0, 1, 2)]
        bank_u = [ps[:, i, :] for i in (3, 4, 5)]
        bank_s, bank_r = ps[:, 6, :], ps[:, 7, :]
        bank_x = [ps[:, 0, :], ps[:, 1, :]]
        bank_h1 = ps[:, 2, :]
        bank_p = [ps[:, 3, :], ps[:, 4, :]]
        bank_b = ps[:, 5, :]
        bank_w = ps[:, 7, :]

        SEMS = """pads_set consts_set edges_in x_in weights_in dve_step ident_ready sel_ready prep_mm
        prep_copied rb_ready first_mm masks_ready ones_set weights_tp weights_tp_copied wk_bias
        bq_ready qk_mm qk_ready bias_ready hot_t_ready t_ready alpha_ready apart_act apart_dve whot_ready
        u_ready u_added row_tp row_ready ends_ready m_end_ready m_end_tp link_m_ready link_tp drop_ready
        shrink_ready shrink_d_ready factor_mm off_ready off_tp below_ready scan_step acc_clear
        x_tp xT_ready un_ready node_step uT_tp uT0_ready uT1_ready projected rows_read h_tp hT_ready
        skip_mm skip_read
        t_mm part1 left_ready part2 part3 var_ready std_ready shift_ready y_ready y_out""".split()
        S = {n: sem(n) for n in SEMS}
        got = [sem(f"got{k}") for k in range(GQ)]
        h_saved = [sem(f"h_saved{k}") for k in range(2)]
        rows_out = [sem(f"rows_out{k}") for k in range(ROW_SETS)]
        dl_in = [sem(f"dl_in{k}") for k in range(2)]

        banks = [bank_s, bank_r]
        block = ctx.enter_context(nc.Block())
        N_EDGE_DMA = 6 + CT
        N_WEIGHT_DMA = 2 * (5 + 2 + G + 2)
        PREP = 3 + ROW_SETS
        NAMES = [("q1", "q2"), ("k1", "k2"), ("v1", "v2"), ("s1", "s2"), ("lin1", "lin2")]
        AHEAD = {"ACT": 2, "DVE": 3}
        SCAN_LINKS = 9

        def chain(eng, s, base=0):
            n = [0]

            def link_(ins):
                n[0] += 1
                ins.then_inc(s, 1)
                eng.wait_ge(s, base + n[0])
            link_.n = n
            return link_

        def rev(t):
            return t[:, ::-1]

        def bins_of(etype, step):
            _, v = nc.values_load_multi_w_load_instructions(
                bin_i[0:1, step:step + UN], engines=[etype], min_val=0, max_val=BINS - 1,
                skip_runtime_bounds_check_because="a step's bin is step - chunk, within 0..24 by the staircase")
            return v

        def slots():
            t = c = 0
            while c < STEPS:
                j = next((j for j in range(NBLK) if 0 <= t - STARTS[j + 1] < S_SLOTS), None)
                k = max((j for j in range(NBLK) if STARTS[j + 1] + S_SLOTS <= t), default=None)
                n = 0
                if k is not None:
                    since, width = t - STARTS[k + 1] - S_SLOTS + 1, (SIZES + (TAIL_SLOTS,))[k + 1]
                    n = min(STARTS[k] + SIZES[k] * since // width, STARTS[k + 1]) - c
                yield (t if t < STEPS else None), ((j, t - STARTS[j + 1]) if j is not None else None), range(c, c + n)
                t, c = t + 1, c + n

        def skip_group(t, late):
            g, rest = divmod(t - STEPS - SKIP_SLOT - late, SKIP_EVERY)
            return g if rest == 0 and 0 <= g < NGR else None

        by_dve = [False] * STEPS
        for a, _, cs in slots():
            for c in cs:
                by_dve[c] = a is None or c % DVE_EVERY == 1

        def made(l, c, dve):
            return l * by_dve.count(dve) + by_dve[:c + 1].count(dve)

        @block.sync
        def _(sp):
            sp.wait_ge(S["pads_set"], 4)
            three = (CT - 1) * P
            for d, t in ((dst_d, dst_i), (src_d, src_i)):
                sp.dma_start(t[:, 0:CT - 1, :],
                             d[0:three * P].rearrange("(t p e) -> p t e", p=P, e=P)).then_inc(S["edges_in"], 16)
                sp.dma_start(t[0:FULL - three, CT - 1, :],
                             d[three * P:FULL * P].rearrange("(p e) -> p e", e=P)).then_inc(S["edges_in"], 16)
                sp.dma_start(t[FULL - three:FULL - three + 1, CT - 1, 0:TAIL],
                             d[FULL * P:EDGES].rearrange("(p e) -> p e", p=1)).then_inc(S["edges_in"], 16)
            with nc.allow_non_contiguous_dma(reason="one value of each chunk"):
                lastcol = dst_d[0:FULL * P].rearrange("(c e) -> c e", e=P)[:, P - 1:P]
                sp.dma_start(prev_i[1:P, 0:1], lastcol[0:P - 1, :]).then_inc(S["edges_in"], 16)
                for t in range(1, CT):
                    n = min(P, CHUNKS - t * P)
                    sp.dma_start(prev_i[0:n, t:t + 1],
                                 lastcol[t * P - 1:t * P - 1 + n, :]).then_inc(S["edges_in"], 16)
            sp.dma_start(x_rows[:, 0:BINS - 1, :],
                         x_d[0:(BINS - 1) * P, :].rearrange("(t p) f -> p t f", p=P)).then_inc(S["x_in"], 16)
            sp.dma_start(x_rows[0:NODES - (BINS - 1) * P, BINS - 1, :],
                         x_d[(BINS - 1) * P:NODES, :]).then_inc(S["x_in"], 16)
            def store_rows(w):
                sp.wait_ge(S["rb_ready"], w + 1)
                for j in range(G * w, min(G * (w + 1), NBLK)):
                    sp.dma_start(dl_d[STARTS[j]:STARTS[j + 1], :], dl_rb[0:SIZES[j], j, :]).then_inc(rows_out[w], 16)
            store_rows(0)
            dl_flat = dl_d.rearrange("(o s) e -> o (s e)", o=1)
            per_layer = STEPS // BC
            for l in range(2):
                for q in range(per_layer):
                    n = l * per_layer + q
                    if l == 0 and q == 2:
                        for w in range(1, ROW_SETS):
                            store_rows(w)
                    if n >= 2:
                        sp.wait_ge(S["hot_t_ready"], n - 1)
                    w = BLOCK_OF[(q + 1) * BC - 1] // G
                    if l == 0 and (q == 0 or w != BLOCK_OF[q * BC - 1] // G):
                        sp.wait_ge(rows_out[w], 16 * len(range(G * w, min(G * (w + 1), NBLK))))
                    sp.dma_start(dl_bc[:, n % 2, :],
                                 dl_flat[:, q * BC * P:(q + 1) * BC * P].to_broadcast([P, BC * P])
                                 ).then_inc(dl_in[n % 2], 16)
                if l == 0:
                    for g in range(NGR):
                        t0, k, _ = group(g)
                        sp.wait_ge(S["rows_read"], g + 1)
                        sp.dma_start(h_d.rearrange("(t p) f -> p t f", p=P)[:, t0:t0 + k, :],
                                     h_out[g % 2][:, 0:k, :]).then_inc(h_saved[g % 2], 16)
            for g in range(NGR):
                t0, k, _ = group(g)
                sp.wait_ge(S["y_ready"], g + 1)
                if t0 + k < BINS:
                    sp.dma_start(out[t0 * P:(t0 + k) * P, :].rearrange("(t p) f -> p t f", p=P),
                                 x_rows[:, t0:t0 + k, :]).then_inc(S["y_out"], 16)
                else:
                    assert k == 1
                    sp.dma_start(out[t0 * P:NODES, :], x_rows[0:NODES - t0 * P, t0, :]).then_inc(S["y_out"], 16)
            sp.wait_ge(S["y_out"], 16 * NGR)

        @block.gpsimd
        def _(pool):
            nc.gpsimd.memset(dst_i[:, CT - 1, :], PAD_NODE).then_inc(S["pads_set"], 1)
            nc.gpsimd.memset(src_i[:, CT - 1, :], 0).then_inc(S["pads_set"], 1)
            nc.gpsimd.memset(prev_i[:, 0:1], 0)
            nc.gpsimd.memset(prev_i[:, 1:CT], PAD_NODE).then_inc(S["pads_set"], 1)
            nc.gpsimd.memset(x_rows[:, BINS - 1, :], 0.0).then_inc(S["pads_set"], 1)

            nc.gpsimd.memset(bias_rows[:, :, :], 0.0).then_inc(S["pads_set"], 1)

            nc.gpsimd.memset(ratio[:, :, :], 1.0)
            nc.gpsimd.memset(ends[:, :, :], 0.0)

            def iota(t, step, n, base_step):
                return nc.gpsimd.iota(t, [[step, n]], base=0, channel_multiplier=base_step,
                                      allow_small_or_imprecise_dtypes=True)
            nc.gpsimd.memset(zeros[:, :], 0.0)
            iota(chunk_f[:, :], P, CT, 1)
            iota(chunk128[:, :], P * P, CT, P)
            iota(step_f, 1, STEPS, 0)
            iota(step128, P, STEPS, 0)
            iota(part128[:, :], 0, 1, P)
            iota(col_f[:, :], 1, P, 0)
            iota(part_f[:, :], 0, 1, 1).then_inc(S["consts_set"], 1)
            nc.gpsimd.memset(gathered[:, :, F:C1], 1.0).then_inc(S["ones_set"], 1)
            pool.wait_ge(S["prep_copied"], 1)
            for l, rows in enumerate((x_d, h_d)):
                if l == 1:
                    for k in range(2):
                        pool.wait_ge(h_saved[k], 16 * len(range(k, NGR, 2)))
                    nc.gpsimd.memset(gathered[:, :, F:C1], 1.0).then_inc(S["ones_set"], 1)
                for t in range(STEPS):
                    n = l * STEPS + t
                    if t >= RING:
                        pool.wait_ge(S["u_ready"], n - RING + 1)
                    if n >= GQ:
                        pool.wait_ge(got[n % GQ], 16 * (n // GQ))
                    nc.gpsimd.indirect_dma_start(
                        out=gathered[:, t % RING, 0:F], out_offset=None, in_=rows[:, :],
                        in_offset=bass.IndirectOffsetOnAxis(ap=src_e[:, t:t + 1], axis=0),
                    ).then_inc(got[n % GQ], 16)

        @block.scalar
        def _(act):
            for l in range(2):
                for n, t in enumerate((wq, wk, wv, wskip, wlin)):
                    act.dma_start(t[:, l, :], A[f"L0_gnn_{NAMES[n][l]}_w"][:, :]).then_inc(S["weights_in"], 16)
            act.wait_ge(S["pads_set"], 5)
            with nc.allow_non_contiguous_dma(reason="biases as columns"):
                for l in range(2):
                    def bias(n):
                        return A[f"L0_gnn_{NAMES[n][l]}_b"]
                    for n, t in enumerate((bq, bk)):
                        act.dma_start(t[:, l, :], bias(n).rearrange("(h k) -> k h", h=HEADS)).then_inc(S["weights_in"], 16)
                    for t in range(G):
                        act.dma_start(bias_rows[HEADS * t:HEADS * (t + 1), l, t * F:(t + 1) * F],
                                      bias(2).rearrange("(h k) -> h k", h=HEADS)).then_inc(S["weights_in"], 16)
                    for n in (3, 4):
                        act.dma_start(bias_rows[BR - 5 + n:BR - 4 + n, l, :].rearrange("o (t k) -> o t k", t=G),
                                      bias(n).rearrange("(o a k) -> o a k", o=1, a=1).to_broadcast([1, G, F])
                                      ).then_inc(S["weights_in"], 16)

            for m in range(4):
                act.wait_ge(S["weights_tp"], m + 1)
                nc.scalar.copy(wqT[:, m, :], bank_t[m % 2][:, 0:F])
                nc.scalar.copy(wkT[:, m, 0:F], bank_t[m % 2][:, F:2 * F]).then_inc(S["weights_tp_copied"], 1)
            def row_set(w):
                act.wait_ge(S["prep_copied"], w + 3)
                nc.scalar.copy(dl_rb[:, G * w:min(G * (w + 1), NBLK), :],
                               dl_r[:, G * w:min(G * (w + 1), NBLK), :]).then_inc(S["rb_ready"], 1)

            row_set(0)
            for m in range(4):
                l, h = divmod(m, 2)
                act.wait_ge(S["qk_mm"], m + 1)
                nc.scalar.mul(qk[:, l, h * C1:(h + 1) * C1], bank_u[m % 2][:, 0:C1], F ** -0.5)
                nc.scalar.mul(qk_bias[:, l, h * C1:(h + 1) * C1], bank_u[m % 2][:, 256:256 + C1],
                              F ** -0.5).then_inc(S["qk_ready"], 1)
            for g in range(NGR):
                t0, k, w = group(g)
                act.wait_ge(S["x_tp"], g + 1)
                nc.scalar.copy(xT[:, t0 * P:t0 * P + w], bank_x[g % 2][:, 0:w]).then_inc(S["xT_ready"], 1)

            def split(l, k):
                n = l * BINS + k
                if k < BINS:
                    if l == 0 and k == MASK_TILE:
                        act.wait_ge(S["masks_ready"], 1)
                        for w in range(ROW_SETS):
                            act.wait_ge(rows_out[w], 16 * len(range(G * w, min(G * (w + 1), NBLK))))
                    if l == 1 and k == MASK_TILE:
                        for i in range(2):
                            act.wait_ge(h_saved[i], 16 * len(range(i, NGR, 2)))
                    act.wait_ge(S["t_mm"], n + 1)
                    nc.scalar.copy(table[:, k, 0, :], bank_u[n % NB][:, 0:CW]).then_inc(S["part1"], 1)
                if k >= 1:
                    act.wait_ge(S["left_ready"], n)
                    nc.scalar.copy(table[:, k - 1, 1, :], left[:, (n - 1) % 2, :]).then_inc(S["part2"], 1)

            def scan(l, j, piece):
                s, r = l * NBLK + j, SIZES[j]
                if piece == 0:
                    act.wait_ge(S["row_tp"], s + 1)
                    nc.scalar.copy(a_row[0:r, :, :].rearrange("p h e -> p (h e)"),
                                   bank_s[0:r, 0:2 * P]).then_inc(S["row_ready"], 1)
                if piece == 4:
                    act.wait_ge(S["drop_ready"], s + 1)
                    nc.scalar.activation(shrink[:, :], drop[:, 1:2], ACT.Exp,
                                         scale=-1.0).then_inc(S["shrink_ready"], 1)
                if piece == 8:
                    act.wait_ge(S["off_tp"], s + 1)
                    nc.scalar.copy(below[:, j % 2, :, 0:r], bank_s[:, 256:256 + 2 * r].rearrange("p (h e) -> p h e", h=HEADS)
                                   ).then_inc(S["below_ready"], 1)

            def far_apart(l, c):
                if l * STEPS + c >= UN:
                    act.wait_ge(S["whot_ready"], l * STEPS + c - UN + 1)
                nc.scalar.activation(apart[:, c % UN, :], col_b[:, :], ACT.Square,
                                     bias=ndl_e[:, c:c + 1]).then_inc(S["apart_act"], 1)

            def weigh(l, c):
                n, j = l * STEPS + c, BLOCK_OF[c]
                if c == STARTS[j]:
                    act.wait_ge(S["below_ready"], l * NBLK + j + 1)
                if by_dve[c]:
                    act.wait_ge(S["apart_dve"], made(l, c, True))
                else:
                    act.wait_ge(S["apart_act"], made(l, c, False))
                if n >= UN:
                    act.wait_ge(S["u_ready"], n - UN + 1)
                for h in range(HEADS):
                    o = c - STARTS[j]
                    last = nc.scalar.activation(whot[:, c % UN, h, :], apart[:, c % UN, :], ACT.Exp, scale=FAR,
                                                bias=below[:, j % 2, h, o:o + 1])
                last.then_inc(S["whot_ready"], 1)

            for l in range(2):
                for k in range(T_AHEAD + 1):
                    split(l, k)
                for t, (a, s, cs) in enumerate(slots()):
                    if l == 0:
                        for w in range(1, ROW_SETS):
                            if a == LATE_ROWS + 2 * w - 1:
                                row_set(w)
                    if a is not None and a + T_AHEAD + 1 <= BINS:
                        split(l, a + T_AHEAD + 1)
                    k = None if a is None else a - LATE_MASKS - 2
                    if k is not None and 0 <= k < BINS:
                        if l == 0 and k == 0:
                            act.wait_ge(S["masks_ready"], 1)
                        nc.scalar.copy(acc[:, k, :], zeros[:, :]).then_inc(S["acc_clear"], 1)
                    if s is not None:
                        scan(l, *s)
                    for c in cs:
                        for k in range(c + AHEAD["ACT"] if c else 0, min(c + AHEAD["ACT"] + 1, STEPS)):
                            if not by_dve[k]:
                                far_apart(l, k)
                        weigh(l, c)
                for g in range(NGR + 3):
                    if g < NGR:
                        t0, k, w = group(g)
                        m = l * NGR + g
                        act.wait_ge(S["uT_tp"], m + 1)
                        if g >= 2:
                            act.wait_ge(S["projected"], m - 1)
                        nc.scalar.copy(ratio[0:k * HEADS, g % 2, :], bank_w[0:k * HEADS, g % 2 * P:(g % 2 + 1) * P])
                        nc.scalar.copy(uT[g % 2][:, 0, 0:w], bank_x[g % 2][:, 0:w]).then_inc(S["uT0_ready"], 1)
                        if l == 1:
                            nc.scalar.copy(uT[g % 2][:, 1, 0:w], bank_h1[:, 0:w]).then_inc(S["uT1_ready"], 1)
                    if l == 0 and 2 <= g < NGR + 2:
                        q = g - 2
                        t0, k, w = group(q)
                        act.wait_ge(S["h_tp"], q + 1)
                        nc.scalar.copy(xT[:, t0 * P:t0 * P + w], bank_b[:, 0:w]).then_inc(S["hT_ready"], 1)
                    if l == 1 and 2 <= g < NGR + 2:
                        t0, k, _ = group(g - 2)
                        act.wait_ge(S["var_ready"], g - 1)
                        nc.scalar.activation(std[:, t0:t0 + k], vare[:, t0:t0 + k], ACT.Sqrt).then_inc(S["std_ready"], 1)
                    if l == 1 and g >= 3:
                        t0, k, _ = group(g - 3)
                        act.wait_ge(S["shift_ready"], g - 2)
                        for t in range(t0, t0 + k):
                            last = nc.scalar.activation(x_rows[:, t, :], x_rows[:, t, :], ACT.Identity,
                                                        scale=rstd[:, t:t + 1], bias=shift[:, t:t + 1])
                        last.then_inc(S["y_ready"], 1)

        @block.tensor
        def _(pe):
            PE = mybir.EngineType.PE
            pe.wait_ge(S["sel_ready"], 1)
            def prepare(r):
                if r >= 2:
                    pe.wait_ge(S["prep_copied"], r - 1)
                b = banks[r % 2]
                if r in (0, 1, PREP - 1):
                    src = {0: src_f, 1: ends}.get(r, dst_f)
                    for t in range(CT):
                        last = nc.tensor.matmul(b[0:ENDS if r == 1 else P, 0:STEPS], src[:, t, :], sel[:, t, :],
                                                start=(t == 0), stop=(t == CT - 1))
                else:
                    for j in range(G * (r - 2), min(G * (r - 1), NBLK)):
                        for t in range(CT):
                            last = nc.tensor.matmul(b[0:SIZES[j], (j % G) * P:(j % G + 1) * P],
                                                    sel[:, t, STARTS[j]:STARTS[j + 1]], dst_f[:, t, :],
                                                    start=(t == 0), stop=(t == CT - 1))
                last.then_inc(S["prep_mm"], 1)

            def x_tiles(g):
                t0, k, w = group(g)
                if g >= 2:
                    pe.wait_ge(S["xT_ready"], g - 1)
                for t in range(k):
                    last = nc.tensor.transpose(bank_x[g % 2][:, t * P:(t + 1) * P], x_rows[:, t0 + t, :], ident[:, :])
                last.then_inc(S["x_tp"], 1)

            prepare(0)
            prepare(1)
            pe.wait_ge(S["ident_ready"], 1)
            pe.wait_ge(S["weights_in"], 16 * N_WEIGHT_DMA)
            for m in range(4):
                l, h = divmod(m, 2)
                if m >= 2:
                    pe.wait_ge(S["weights_tp_copied"], m - 1)
                nc.tensor.transpose(bank_t[m % 2][:, 0:F], wq[:, l, h * F:(h + 1) * F], ident[:, :])
                nc.tensor.transpose(bank_t[m % 2][:, F:2 * F], wk[:, l, h * F:(h + 1) * F],
                                    ident[:, :]).then_inc(S["weights_tp"], 1)
            prepare(2)
            pe.wait_ge(S["wk_bias"], 1)
            for m in range(4):
                l, h = divmod(m, 2)
                pe.wait_ge(S["weights_tp_copied"], m + 1)
                if m >= 2:
                    pe.wait_ge(S["qk_ready"], m - 1)
                nc.tensor.matmul(bank_u[m % 2][:, 0:C1], wqT[:, m, :], wkT[:, m, :], start=True, stop=True)
                pe.wait_ge(S["bq_ready"], m + 1)
                nc.tensor.matmul(bank_u[m % 2][:, 256:256 + C1], bq_wide, wkT[:, m, :],
                                 start=True, stop=True).then_inc(S["qk_mm"], 1)
            pe.wait_ge(S["x_in"], 32)
            for g in range(NGR):
                x_tiles(g)

            def late_prepare(a):
                for w in range(1, ROW_SETS):
                    if a == LATE_ROWS + 2 * (w - 1):
                        prepare(2 + w)
                if a == LATE_DST - 1:
                    prepare(PREP - 1)
                if a == LATE_MASKS:
                    pe.wait_ge(S["prep_copied"], PREP)
                    nc.tensor.matmul(bank_r[:, 0:STEPS], ones[0:1, :], firsts[0:1], start=True, stop=True
                                     ).then_inc(S["first_mm"], 1)

            def make_t(l, k):
                n = l * BINS + k
                if l == 0 and k == 0:
                    pe.wait_ge(S["qk_ready"], 4)
                    pe.wait_ge(S["bias_ready"], 1)
                if k % G == 0:
                    pe.wait_ge(S[("xT_ready", "hT_ready")[l]], k // G + 1)
                if k == 0 and l == 1:
                    pe.wait_ge(S["rows_read"], NGR)
                    pe.wait_ge(S["hT_ready"], NGR)
                if n >= NB:
                    pe.wait_ge(S["left_ready"], n - NB + 1)
                nc.tensor.matmul(bank_u[n % NB][:, 0:CW], xT[:, k * P:(k + 1) * P], qk[:, l, :], start=True, stop=False)
                nc.tensor.matmul(bank_u[n % NB][:, 0:CW], ones_b[:, :], bias3[:, l, :],
                                 start=False, stop=True).then_inc(S["t_mm"], 1)

            def make_skip(l, g):
                t0, k, _ = group(g)
                pe.wait_ge(S["alpha_ready"], (l + 1) * STEPS)
                if g >= 2:
                    pe.wait_ge(S["skip_read"], l * NGR + g - 1)
                for t in range(k):
                    last = nc.tensor.matmul(bank_x[g % 2][:, t * P:(t + 1) * P], xT[:, (t0 + t) * P:(t0 + t + 1) * P],
                                            wskip[:, l, :], start=True, stop=True)
                last.then_inc(S["skip_mm"], 1)

            def step_t(l, t, b):
                n = l * STEPS + t
                if t % BC == 0:
                    pe.wait_ge(S["hot_t_ready"], n // BC + 1)
                if n >= NB:
                    pe.wait_ge(S["alpha_ready"], n - NB + 1)
                for part in range(3):
                    last = nc.tensor.matmul(bank_t[n % NB][:, 0:CW], hot_t[:, n // BC % 2, t % BC, :],
                                            table[:, bass.ds(b, 1), part, :].rearrange("p o c -> p (o c)"),
                                            start=(part == 0), stop=(part == 2))
                last.then_inc(S["t_ready"], 1)

            def step_u(l, c):
                n = l * STEPS + c
                if n >= NB:
                    pe.wait_ge(S["u_added"], n - NB + 1)
                pe.wait_ge(S["whot_ready"], n + 1)
                for h in range(HEADS):
                    last = nc.tensor.matmul(bank_u[n % NB][:, h * C1:(h + 1) * C1], whot[:, c % UN, h, :],
                                            gathered[:, c % RING, :], start=True, stop=True)
                last.then_inc(S["u_ready"], 1)

            def scan(l, j, piece):
                s, r = l * NBLK + j, SIZES[j]
                if piece == 0:
                    pe.wait_ge(S["alpha_ready"], l * STEPS + STARTS[j + 1])
                    for h in range(HEADS):
                        last = nc.tensor.transpose(bank_s[0:r, h * P:(h + 1) * P], alpha[:, j % 2, h, 0:r], ident[:, :])
                    last.then_inc(S["row_tp"], 1)
                if piece == 2:
                    pe.wait_ge(S["m_end_ready"], s + 1)
                    for n in range(2):
                        last = nc.tensor.transpose(bank_r[0:2, n * 64:n * 64 + r], m_end[0:r, 2 * n:2 * n + 2],
                                                   ident[0:r, 0:r])
                    last.then_inc(S["m_end_tp"], 1)
                if piece == 4:
                    pe.wait_ge(S["link_m_ready"], s + 1)
                    for n in range(2):
                        last = nc.tensor.transpose(bank_r[0:r, 256 + 2 * n:258 + 2 * n], link_m[:, n, 0:r],
                                                   ident[0:2, 0:2])
                    last.then_inc(S["link_tp"], 1)
                if piece == 6:
                    pe.wait_ge(S["shrink_d_ready"], s + 1)
                    nc.tensor.matmul(bank_r[:, 300:302], ones[:, :], shrink_d[:, :],
                                     start=True, stop=True).then_inc(S["factor_mm"], 1)
                if piece == 7:
                    pe.wait_ge(S["off_ready"], s + 1)
                    for h in range(HEADS):
                        last = nc.tensor.transpose(bank_s[:, 256 + h * r:256 + (h + 1) * r], a_off[0:r, h, :],
                                                   ident[0:r, 0:r])
                    last.then_inc(S["off_tp"], 1)

            for l in range(2):
                for k in range(T_AHEAD + 2):
                    make_t(l, k)
                b = {}
                for t, (a, s, cs) in enumerate(slots()):
                    if l == 0:
                        late_prepare(a)
                    if a is not None:
                        if a + T_AHEAD + 2 < BINS:
                            make_t(l, a + T_AHEAD + 2)
                        for k in range(a + PE_AHEAD if a else 0, min(a + PE_AHEAD + 1, STEPS)):
                            if k % UN == 0:
                                b = bins_of(PE, k)
                            if k < BINS:
                                pe.wait_ge(S["part3"], l * BINS + k + 1)
                            step_t(l, k, b[k % UN])
                    if s is not None:
                        scan(l, *s)
                    for c in cs:
                        step_u(l, c)
                    if skip_group(t, 0) is not None:
                        make_skip(l, skip_group(t, 0))
                for g in range(NGR + 2):
                    if g < NGR:
                        t0, k, w = group(g)
                        m = l * NGR + g
                        if g == 0:
                            pe.wait_ge(S["skip_read"], (l + 1) * NGR)
                        pe.wait_ge(S["un_ready"], m + 1)
                        if g >= 1:
                            pe.wait_ge(S["uT0_ready"], m)
                            pe.wait_ge(S["uT1_ready"], m)
                        nc.tensor.transpose(bank_w[0:k * HEADS, g % 2 * P:(g % 2 + 1) * P],
                                            u_n[g % 2][:, 0:k * HEADS, F], ident[:, :])
                        for h in range(HEADS):
                            for t in range(k):
                                last = nc.tensor.transpose((bank_x[g % 2], bank_h1)[h][:, t * P:(t + 1) * P],
                                                           u_n[g % 2][:, t * HEADS + h, 0:F], ident[:, :])
                        last.then_inc(S["uT_tp"], 1)
                    if 1 <= g <= NGR:
                        q = g - 1
                        t0, k, w = group(q)
                        m = l * NGR + q
                        if q >= 2:
                            pe.wait_ge(S["rows_read"], m - 1)
                        pe.wait_ge(S["uT0_ready"], m + 1)
                        pe.wait_ge(S["uT1_ready"], m + 1)
                        nc.tensor.matmul(bank_p[q % 2][:, 0:w], ratio[:, q % 2, :], bias_rows[:, l, 0:w],
                                         start=True, stop=False)
                        for t in range(k):
                            o = bank_p[q % 2][:, t * P:(t + 1) * P]
                            for h in range(HEADS):
                                last = nc.tensor.matmul(o, uT[q % 2][:, h, t * P:(t + 1) * P],
                                                        wv[:, l, h * F:(h + 1) * F], start=False,
                                                        stop=(t == k - 1 and h == HEADS - 1))
                        last.then_inc(S["projected"], 1)
                    if l == 0 and g >= 2:
                        q = g - 2
                        t0, k, w = group(q)
                        pe.wait_ge(S["rows_read"], q + 1)
                        if q >= 1:
                            pe.wait_ge(S["hT_ready"], q)
                        for t in range(k):
                            last = nc.tensor.transpose(bank_b[:, t * P:(t + 1) * P], h_out[q % 2][:, t, :], ident[:, :])
                        last.then_inc(S["h_tp"], 1)

        @block.vector
        def _(dve):
            DVE = mybir.EngineType.DVE
            V = nc.vector
            step = chain(dve, S["dve_step"])
            dve.wait_ge(S["consts_set"], 1)
            V.memset(dl_r, 0.0)
            step(V.memset(ones_b[:, :], 0.0))
            for k in (0, 32, 64):
                V.memset(ones_b[k:k + 1, :], 1.0)
            V.tensor_scalar(ident[:, :], col_f[:, :], part_f[:, 0:1], None, ALU.is_equal).then_inc(S["ident_ready"], 1)

            dve.wait_ge(S["edges_in"], 16 * N_EDGE_DMA)
            V.tensor_scalar(lastbin_i[:, :], dst_i[:, :, P - 1], 7, None, ALU.arith_shift_right)
            V.tensor_scalar(prevbin_i[:, :], prev_i[:, :], 7, None, ALU.arith_shift_right)
            step(V.tensor_copy(src_f[:, :, :], src_i[:, :, :]))
            V.tensor_tensor(key[:, :], lastbin_i[:, :], chunk_f[:, :], ALU.add)
            V.scalar_tensor_tensor(out=keyprev[:, :], in0=prevbin_i[:, :], scalar=-1.0, in1=chunk_f[:, :],
                                   op0=ALU.add, op1=ALU.add)
            for t in range(CT):
                last = V.tensor_scalar(dst_f[:, t, :], dst_i[:, t, :], chunk128[:, t:t + 1], None, ALU.add)
            step(last)
            for t in range(CT):
                last = V.tensor_scalar(before[:, t, :], step_f, key[:, t:t + 1], None, ALU.is_le)
            step(last)
            V.tensor_copy(ends[:, :, 0:2], dst_f[:, :, 0:1].to_broadcast([P, CT, 2]))
            V.tensor_copy(ends[:, :, 32:34], dst_f[:, :, P - 1:P].to_broadcast([P, CT, 2]))
            V.tensor_copy(ends[:, :, 64], chunk_f[:, :])
            for t in range(CT):
                last = V.scalar_tensor_tensor(out=sel[:, t, :], in0=step_f, scalar=keyprev[:, t:t + 1],
                                              in1=before[:, t, :], op0=ALU.is_gt, op1=ALU.mult)
            last.then_inc(S["sel_ready"], 1)
            V.tensor_copy(col_b[:, :], col_f[:, :])
            V.tensor_scalar(ncol_b[:, :], col_f[:, :], -1.0, None, ALU.mult)
            V.memset(ones[:, :], 1.0)
            V.memset(run_b[:, :], -BIG)
            V.memset(link[:, :], 0.0)
            V.memset(seg_f[:, :, 0:1], 0.0)
            V.memset(seg_b[:, :, 0:1], 0.0)

            def copied(r, ins):
                ins.then_inc(S["prep_copied"], 1)
            dve.wait_ge(S["prep_mm"], 1)
            copied(0, V.tensor_copy(src_e[:, :], bank_s[:, 0:STEPS]))
            dve.wait_ge(S["weights_in"], 16 * N_WEIGHT_DMA)
            V.tensor_copy(wkT[:, :, F], bk[:, :, :].rearrange("p l h -> p (l h)")).then_inc(S["wk_bias"], 1)
            V.tensor_copy(bq_wide, bq[:, 0, 0:1].to_broadcast([P, P])).then_inc(S["bq_ready"], 1)
            dve.wait_ge(S["prep_mm"], 2)
            V.tensor_tensor(bin_i[:, :], step_f[0:1], bank_r[64:65, 0:STEPS], ALU.subtract)
            V.tensor_tensor(firsts, bank_r[0:2, 0:STEPS], step128[0:2], ALU.subtract)
            copied(1, V.tensor_tensor(lasts, bank_r[32:34, 0:STEPS], step128[0:2], ALU.subtract))

            def row_set(w):
                dve.wait_ge(S["prep_mm"], w + 3)
                for j in range(G * w, min(G * (w + 1), NBLK)):
                    last = V.tensor_scalar(dl_r[0:SIZES[j], j, :],
                                           banks[w % 2][0:SIZES[j], (j % G) * P:(j % G + 1) * P],
                                           part128[0:SIZES[j], 0:1], float(STARTS[j] * P), ALU.subtract, ALU.subtract)
                copied(2 + w, last)
            row_set(0)
            for m in range(1, 4):
                dve.wait_ge(S["qk_mm"], m)
                V.tensor_copy(bq_wide, bq[:, m // 2, m % 2:m % 2 + 1].to_broadcast([P, P])
                              ).then_inc(S["bq_ready"], 1)
            V.tensor_tensor(wskip[:, :, :], wskip[:, :, :], wlin[:, :, :], ALU.add)
            dve.wait_ge(S["qk_ready"], 4)
            step(V.tensor_copy(bias3[0:65, :, :], qk_bias[0:65]))
            step(V.tensor_tensor(qk_bias[0:65], qk_bias[0:65], bias3[0:65, :, :], ALU.subtract))
            V.tensor_copy(bias3[32:33, :, :], qk_bias[32:33])
            step(V.tensor_copy(bias3[64:65, :, :], qk_bias[64:65]))
            step(V.tensor_tensor(qk_bias[64:65], qk_bias[64:65], bias3[64:65, :, :], ALU.subtract))
            V.tensor_copy(bias3[64:65, :, :], qk_bias[64:65]).then_inc(S["bias_ready"], 1)

            def split(l, k):
                n = l * BINS + k
                if k < BINS:
                    dve.wait_ge(S["part1"], n + 1)
                    if n >= 2:
                        dve.wait_ge(S["part3"], n - 1)
                    V.tensor_tensor(left[:, n % 2, :], bank_u[n % NB][:, 0:CW], table[:, k, 0, :],
                                    ALU.subtract).then_inc(S["left_ready"], 1)
                if k >= 1:
                    dve.wait_ge(S["part2"], n)
                    V.tensor_tensor(table[:, k - 1, 2, :], left[:, (n - 1) % 2, :], table[:, k - 1, 1, :],
                                    ALU.subtract).then_inc(S["part3"], 1)

            def penalty(o, i):
                return V.tensor_scalar(o, i, 1.0, BIG, ALU.subtract, ALU.mult)

            def masks():
                V.tensor_tensor(same[:, :, 0:P - 1], dl_r[:, :, 1:P], dl_r[:, :, 0:P - 1], ALU.is_equal)
                V.tensor_tensor(in_last[:, :, :], dl_r, dl_r[:, :, P - 1:P].to_broadcast([BLK, NBLK, P]), ALU.is_equal)
                V.tensor_tensor(in_first[:, :, :], dl_r, dl_r[:, :, 0:1].to_broadcast([BLK, NBLK, P]), ALU.is_equal)
                V.tensor_tensor(link[:, 1:STEPS], lasts[:, 0:STEPS - 1], firsts[:, 1:STEPS], ALU.is_equal)
                step(V.tensor_tensor(single, firsts, lasts, ALU.is_equal))
                penalty(seg_f[:, :, 1:P], same[:, :, 0:P - 1])
                penalty(seg_b[:, :, 1:P], same[:, :, P - 2::-1])
                penalty(linkneg[:, :], link[:, :])
                V.tensor_tensor(carry_f[:, :], link[:, 0:STEPS], single, ALU.mult)
                step(V.tensor_tensor(joined, link[:, 1:STEPS + 1], single, ALU.mult))
                penalty(in_last[:, :, :], in_last[:, :, :])
                penalty(in_first[:, :, :], in_first[:, :, :])
                penalty(carry_f[:, :], carry_f[:, :])
                step(penalty(carry_b[:, :], rev(joined)))

            def first_hots():
                dve.wait_ge(S["first_mm"], 1)
                for j in range(NBLK):
                    last = V.tensor_scalar(first_hot[:, j:j + 1], bank_r[:, STARTS[j]:STARTS[j] + 1], part_f[:, 0:1], None,
                                           ALU.is_equal)
                last.then_inc(S["masks_ready"], 1)

            def late_prepare(a):
                for w in range(1, ROW_SETS):
                    if a == LATE_ROWS + 2 * w - 1:
                        row_set(w)
                if a == LATE_DST:
                    dve.wait_ge(S["prep_mm"], PREP)
                    copied(PREP - 1, V.tensor_tensor(ndl_e[:, :], step128, banks[(PREP - 1) % 2][:, 0:STEPS],
                                                     ALU.subtract))
                if a == LATE_MASKS:
                    dve.wait_ge(S["prep_copied"], PREP)
                    masks()
                if a == LATE_MASKS + 1:
                    first_hots()

            def one_hot_t(q):
                dve.wait_ge(dl_in[q % 2], 16 * (q // 2 + 1))
                V.tensor_scalar(hot_t[:, q % 2, :, :].rearrange("p k e -> p (k e)"), dl_bc[:, q % 2, :],
                                part_f[:, 0:1], None, ALU.is_equal).then_inc(S["hot_t_ready"], 1)

            def step_alpha(l, t):
                n, j = l * STEPS + t, BLOCK_OF[t]
                if n >= 2:
                    dve.wait_ge(S["alpha_ready"], n - 1)
                dve.wait_ge(got[n % GQ], 16 * (n // GQ + 1))
                dve.wait_ge(S["t_ready"], n + 1)
                for h in range(HEADS):
                    last = V.scalar_tensor_tensor(
                        out=junk[:, t % 2, h, :], in0=bank_t[n % NB][:, h * C1:(h + 1) * C1], scalar=1.0,
                        in1=gathered[:, t % RING, :], op0=ALU.mult, op1=ALU.mult,
                        accum_out=alpha[:, j % 2, h, t - STARTS[j]:t - STARTS[j] + 1])
                last.then_inc(S["alpha_ready"], 1)

            def far_apart(l, c):
                n = l * STEPS + c
                if n >= UN:
                    dve.wait_ge(S["whot_ready"], n - UN + 1)
                V.tensor_scalar(apart[:, c % UN, :], ncol_b[:, :], ndl_e[:, c:c + 1], None,
                                ALU.not_equal).then_inc(S["apart_dve"], 1)

            def read_skip(l, g):
                t0, k, w = group(g)
                dve.wait_ge(S["skip_mm"], l * NGR + g + 1)
                product = bank_x[g % 2][:, 0:w].rearrange("p (t f) -> p t f", t=k)
                if l == 0:
                    V.tensor_copy(skip[:, t0:t0 + k, :], product).then_inc(S["skip_read"], 1)
                else:
                    rows = x_rows[:, t0:t0 + k, :]
                    V.tensor_tensor(rows, rows, product, ALU.add).then_inc(S["skip_read"], 1)

            def step_add(l, c, b):
                n = l * STEPS + c
                if n >= 1:
                    dve.wait_ge(S["u_added"], n)
                dve.wait_ge(S["u_ready"], n + 1)
                bin_acc = acc[:, bass.ds(b, 1), :].rearrange("p o c -> p (o c)")
                V.tensor_tensor(bin_acc, bank_u[n % NB][:, 0:CW], bin_acc, ALU.add).then_inc(S["u_added"], 1)

            def scan(l, j, piece):
                s = l * NBLK + j
                ln = chain(dve, S["scan_step"], s * SCAN_LINKS + {1: 0, 3: 1, 5: 4, 6: 6, 7: 7}.get(piece, 0))
                p0, r = STARTS[j], SIZES[j]
                if piece == 1:
                    dve.wait_ge(S["row_ready"], s + 1)
                    for n, mask in enumerate((in_last, in_first)):
                        last = V.tensor_tensor(a_end[0:r, 2 * n:2 * n + 2, :], a_row[0:r, :, :],
                                               mask[0:r, j:j + 1, :].to_broadcast([r, HEADS, P]), ALU.add)
                    ln(last)
                    V.tensor_reduce(m_end[0:r, :], a_end[0:r, :, :], AX, ALU.max).then_inc(S["m_end_ready"], 1)
                if piece == 3:
                    dve.wait_ge(S["m_end_tp"], s + 1)
                    V.tensor_tensor_scan(run_f[:, 1:r + 1], carry_f[:, p0:p0 + r], bank_r[0:2, 0:r],
                                         run_f[:, 0:1], ALU.add, ALU.max)
                    ln(V.tensor_tensor_scan(rev(run_b[:, BLK - r:BLK]), carry_b[:, STEPS - p0 - r:STEPS - p0],
                                            rev(bank_r[0:2, 64:64 + r]),
                                            -BIG, ALU.add, ALU.max))
                    V.tensor_tensor(link_m[:, 0, 0:r], run_f[:, 0:r], linkneg[:, p0:p0 + r], ALU.add)
                    V.tensor_tensor(link_m[:, 1, 0:r], run_b[:, BLK - r + 1:BLK + 1], linkneg[:, p0 + 1:p0 + r + 1],
                                    ALU.add).then_inc(S["link_m_ready"], 1)
                    ln(V.scalar_tensor_tensor(out=drop[:, 0:1], in0=run_b[:, BLK - r:BLK - r + 1], scalar=run_f[:, 0:1],
                                              in1=run_f[:, 0:1], op0=ALU.max, op1=ALU.subtract))
                    V.tensor_tensor(drop[:, 1:2], drop[:, 0:1], link[:, p0:p0 + 1], ALU.mult).then_inc(S["drop_ready"], 1)
                    ln(V.tensor_copy(run_f[:, 0:1], run_f[:, r:r + 1]))
                if piece == 5:
                    dve.wait_ge(S["link_tp"], s + 1)
                    ln(V.tensor_copy(link_c[0:r, :], bank_r[0:r, 256:260]))
                    dve.wait_ge(S["shrink_ready"], s + 1)
                    V.tensor_scalar(shrink_d[:, :], ident[0:2, 0:2], shrink[:, 0:1], None,
                                    ALU.mult).then_inc(S["shrink_d_ready"], 1)
                    for h in range(HEADS):
                        V.tensor_tensor_scan(max_f[0:r, h, :], seg_f[0:r, j, :], a_row[0:r, h, :],
                                             link_c[0:r, h:h + 1], ALU.add, ALU.max)
                        last = V.tensor_tensor_scan(rev(max_b[0:r, h, :]), seg_b[0:r, j, :], rev(a_row[0:r, h, :]),
                                                    link_c[0:r, 2 + h:3 + h], ALU.add, ALU.max)
                    last.then_inc(S["scan_step"], 1)
                if piece == 6:
                    dve.wait_ge(S["scan_step"], s * SCAN_LINKS + 6)
                    ln(V.tensor_tensor(max_s[0:r, :, :], max_f[0:r, :, :], max_b[0:r, :, :], ALU.max))
                    V.tensor_tensor(a_off[0:r, :, :], a_row[0:r, :, :], max_s[0:r, :, :], ALU.subtract
                                    ).then_inc(S["off_ready"], 1)
                if piece == 7:
                    dve.wait_ge(S["factor_mm"], s + 1)
                    ln(V.tensor_scalar(shrink_1[:, :], bank_r[:, 300:302], 1.0, None, ALU.subtract))
                    V.tensor_scalar(factor[:, :], shrink_1[:, :], first_hot[:, j:j + 1], 1.0,
                                    ALU.mult, ALU.add).then_inc(S["scan_step"], 1)

            def rescale(l, j, b):
                s = l * NBLK + j
                dve.wait_ge(S["scan_step"], (s + 1) * SCAN_LINKS)
                if s > 0:
                    dve.wait_ge(S["u_added"], l * STEPS + STARTS[j])
                for h in range(HEADS):
                    o = acc[:, bass.ds(b, 1), h * C1:(h + 1) * C1].rearrange("p o c -> p (o c)")
                    last = V.tensor_scalar(o, o, factor[:, h:h + 1], None, ALU.mult)
                last.then_inc(S["ends_ready"], 1)
                dve.wait_ge(S["ends_ready"], s + 1)

            step(V.memset(run_f[:, 0:1], -BIG))
            for l in range(2):
                if l == 1:
                    step(V.memset(run_f[:, 0:1], -BIG))
                for k in range(T_AHEAD + 1):
                    split(l, k)
                dve.wait_ge(S["ones_set"], l + 1)
                q0 = l * (STEPS // BC)
                one_hot_t(q0)
                for t, (a, s, cs) in enumerate(slots()):
                    if l == 0:
                        late_prepare(a)
                    if a is not None:
                        if a + T_AHEAD + 1 <= BINS:
                            split(l, a + T_AHEAD + 1)
                        if a % BC == 1 and a // BC + 1 < STEPS // BC:
                            one_hot_t(q0 + a // BC + 1)
                        step_alpha(l, a)
                    if s is not None:
                        scan(l, *s)
                    for c in cs:
                        if c == 0:
                            dve.wait_ge(S["acc_clear"], (l + 1) * BINS)
                        else:
                            step_add(l, c - 1, b[(c - 1) % UN])
                        for k in range(c + AHEAD["DVE"] if c else 0, min(c + AHEAD["DVE"] + 1, STEPS)):
                            if by_dve[k]:
                                far_apart(l, k)
                        if c % UN == 0:
                            b = bins_of(DVE, c)
                        if c in STARTS:
                            rescale(l, BLOCK_OF[c], b[c % UN])
                    if skip_group(t, 1) is not None:
                        read_skip(l, skip_group(t, 1))
                step_add(l, STEPS - 1, b[UN - 1])
                dve.wait_ge(S["u_added"], (l + 1) * STEPS)
                dve.wait_ge(S["skip_read"], (l + 1) * NGR)

                def normalise(g):
                    t0, k, _ = group(g)
                    m = l * NGR + g
                    sums = acc[:, t0:t0 + k, :].rearrange("p t (h c) -> p (t h) c", h=HEADS)
                    d, r = den[:, g, 0:2 * k], rden[:, g, 0:2 * k]
                    if g >= 2:
                        dve.wait_ge(S["uT_tp"], m - 1)
                    ln = chain(dve, S["node_step"], 2 * m)
                    ln(V.tensor_scalar(d, sums[:, :, F], 1e-16, float(HEADS), ALU.add, ALU.mult))
                    ln(V.reciprocal(r, d))
                    V.tensor_tensor(u_n[g % 2][:, 0:2 * k, :], sums,
                                    r.rearrange("p (t o) -> p t o", o=1).to_broadcast([P, 2 * k, C1]),
                                    ALU.mult).then_inc(S["un_ready"], 1)
                normalise(0)
                for g in range(NGR + 3):
                    if g + 1 < NGR:
                        normalise(g + 1)
                    if l == 0 and g < NGR:
                        t0, k, w = group(g)
                        dve.wait_ge(S["uT_tp"], l * NGR + g + 1)
                        if g >= 2:
                            dve.wait_ge(S["projected"], l * NGR + g - 1)
                        V.tensor_copy(uT[g % 2][:, 1, 0:w], bank_h1[:, 0:w]).then_inc(S["uT1_ready"], 1)
                    if 2 <= g < NGR + 2:
                        q = g - 2
                        t0, k, w = group(q)
                        dve.wait_ge(S["projected"], l * NGR + q + 1)
                        if l == 0:
                            if q >= 2:
                                dve.wait_ge(h_saved[q % 2], 16 * (q // 2))
                                dve.wait_ge(S["h_tp"], q - 1)
                            V.tensor_tensor(h_out[q % 2][:, 0:k, :], skip[:, t0:t0 + k, :],
                                            bank_p[q % 2][:, 0:w].rearrange("p (t f) -> p t f", t=k),
                                            ALU.add).then_inc(S["rows_read"], 1)
                        else:
                            rows = x_rows[:, t0:t0 + k, :]
                            V.tensor_tensor(rows, rows, bank_p[q % 2][:, 0:w].rearrange("p (t f) -> p t f", t=k),
                                            ALU.add).then_inc(S["rows_read"], 1)
                            dve.wait_ge(S["rows_read"], l * NGR + q + 1)
                            for t in range(t0, t0 + k):
                                last = V.bn_stats(stats[:, t, :], x_rows[:, t, :])
                            step(last)
                            for t in range(t0, t0 + k):
                                last = V.bn_aggr(mv[:, t, :], stats[:, t, :])
                            step(last)
                            V.tensor_scalar(vare[:, t0:t0 + k], mv[:, t0:t0 + k, 1], EPS_LN, None,
                                            ALU.add).then_inc(S["var_ready"], 1)
                    if l == 1 and g >= 3:
                        t0, k, _ = group(g - 3)
                        dve.wait_ge(S["std_ready"], g - 2)
                        step(V.reciprocal(rstd[:, t0:t0 + k], std[:, t0:t0 + k]))
                        V.scalar_tensor_tensor(out=shift[:, t0:t0 + k], in0=mv[:, t0:t0 + k, 0], scalar=-1.0,
                                               in1=rstd[:, t0:t0 + k], op0=ALU.mult, op1=ALU.mult
                                               ).then_inc(S["shift_ready"], 1)


_INS = ["x", "src", "dst"] + [f"L0_gnn_{n}_{k}" for n in ("q1", "k1", "v1", "s1", "q2", "k2", "v2", "s2", "lin1", "lin2")
                              for k in ("w", "b")]


def kernel(**inputs):
    import numpy as _np
    import concourse.bacc as _bacc
    from concourse import mybir as _mybir
    from concourse.bass_utils import run_bass_kernel_spmd as _run

    nc = _bacc.Bacc("TRN2", target_bir_lowering=False, num_devices=1)
    arrays, args = {}, {}
    for name in _INS:
        a = _np.ascontiguousarray(inputs[name])
        arrays[f"in_{name}"] = a
        args[name] = nc.dram_tensor(f"in_{name}", a.shape, _mybir.dt.from_np(a.dtype), kind="ExternalInput").ap()
    out = nc.dram_tensor("out", (NODES, F), _mybir.dt.float32, kind="ExternalOutput").ap()
    program(nc, args, out)
    r = _run(nc, [arrays], core_ids=[0])
    return r.results[0]["out"]
```
